# Optimizing a Trainium2 kernel written in Bass

```python
import numpy as np
import jax
import jax.numpy as jnp

def _softmax(x, axis=-1):
    return jax.nn.softmax(x, axis=axis)

def _gelu(x):
    return jax.nn.gelu(x, approximate=True)

def _silu(x):
    return jax.nn.silu(x)

def _sigmoid(x):
    return jax.nn.sigmoid(x)

def _layernorm(x, axis=-1, eps=1e-05):
    m = jnp.mean(x, axis=axis, keepdims=True)
    v = jnp.var(x, axis=axis, keepdims=True)
    return (x - m) / jnp.sqrt(v + eps)

def _scatter_add(tgt, idx, src, axis=0):
    return tgt.at[idx].add(src)

def _segment_sum(src, seg, n):
    return jax.ops.segment_sum(src, seg, n)
kernel_name = 'mk_gnn_resnorm_d2_gnn_r64_7c2105'

def setup_inputs(seed: int=0):
    np.random.seed(seed)
    _w = jnp.asarray

    def _rec_inputs():
        import jax
        import jax.numpy as jnp
        _gk = jax.random.key(seed)
        x = -0.000202 + 1 * jax.random.normal(jax.random.fold_in(_gk, 1), (100000, 128), jnp.float32)
        src = jax.random.randint(jax.random.fold_in(_gk, 2), (25000,), 0, 100000, jnp.int32)
        dst = jnp.minimum((100000 * jax.random.uniform(jax.random.fold_in(_gk, 3), (25000,)) ** 2.0).astype(jnp.int32), 99999)
        _o = jnp.argsort(dst, stable=True)
        src = src[_o]
        dst = dst[_o]
        edge_attr_128 = 2.93046e-05 + 1.00006 * jax.random.normal(jax.random.fold_in(_gk, 11), (25000, 128), jnp.float32)
        edge_type_16 = jax.random.randint(jax.random.fold_in(_gk, 13), (25000,), 0, 16, jnp.int32)
        return (x, src, dst, edge_attr_128, edge_type_16)
    x, src, dst, edge_attr_128, edge_type_16 = _rec_inputs()

    def _L0_gnn_setup():
        import jax, jax.numpy as jnp
        import numpy as np
        N_NODES = 50000
        N_EDGES = 25000
        D_IN = 128
        D_OUT = 128
        N_REL = 16
        key = jax.random.key(seed)
        k1, k2, k3, k4, k5 = jax.random.split(key, 5)
        node_features = jax.random.normal(k1, (N_NODES, D_IN), dtype=jnp.float32)
        edge_index = jax.random.randint(k2, (2, N_EDGES), 0, N_NODES, dtype=jnp.int64)
        edge_type = jax.random.randint(k3, (N_EDGES,), 0, N_REL, dtype=jnp.int64)
        W_rel = jax.random.normal(k4, (N_REL, D_IN, D_OUT), dtype=jnp.float32) / np.sqrt(D_IN)
        W_root = jax.random.normal(k5, (D_IN, D_OUT), dtype=jnp.float32) / np.sqrt(D_IN)
        bias = jnp.zeros((D_OUT,), dtype=jnp.float32)
        return {'node_features': node_features, 'edge_index': edge_index, 'edge_type': edge_type, 'W_rel': W_rel, 'W_root': W_root, 'bias': bias}
    _L0_gnn_all = _L0_gnn_setup()
    _L0_gnn_in = {k: v for k, v in _L0_gnn_all.items() if k in ('W_rel', 'W_root', 'bias')}
    del _L0_gnn_all

    def _L1_gnn_setup():
        import jax, jax.numpy as jnp
        import numpy as np
        N_NODES = 50000
        N_EDGES = 10000
        HID = 128
        LN_EPS = 1e-05

        def _layer_norm(h, gamma, beta):
            mu = jnp.mean(h, axis=-1, keepdims=True)
            var = jnp.mean(jnp.square(h - mu), axis=-1, keepdims=True)
            return (h - mu) * jax.lax.rsqrt(var + LN_EPS) * gamma + beta
        key = jax.random.key(seed)
        ks = jax.random.split(key, 8)
        x = jax.random.normal(ks[0], (N_NODES, HID), dtype=jnp.float32)
        edge_index = jax.random.randint(ks[1], (2, N_EDGES), 0, N_NODES, dtype=jnp.int64)
        edge_attr = jax.random.normal(ks[2], (N_EDGES, HID), dtype=jnp.float32)
        msg_W1 = jax.random.normal(ks[3], (3 * HID, HID), dtype=jnp.float32) / np.sqrt(3 * HID)
        msg_b1 = jnp.zeros((HID,), dtype=jnp.float32)
        msg_W2 = jax.random.normal(ks[4], (HID, HID), dtype=jnp.float32) / np.sqrt(HID)
        msg_b2 = jnp.zeros((HID,), dtype=jnp.float32)
        upd_W1 = jax.random.normal(ks[5], (2 * HID, HID), dtype=jnp.float32) / np.sqrt(2 * HID)
        upd_b1 = jnp.zeros((HID,), dtype=jnp.float32)
        upd_W2 = jax.random.normal(ks[6], (HID, HID), dtype=jnp.float32) / np.sqrt(HID)
        upd_b2 = jnp.zeros((HID,), dtype=jnp.float32)
        ln_gamma = jnp.ones((HID,), dtype=jnp.float32)
        ln_beta = jnp.zeros((HID,), dtype=jnp.float32)
        return {'x': x, 'edge_index': edge_index, 'edge_attr': edge_attr, 'msg_W1': msg_W1, 'msg_b1': msg_b1, 'msg_W2': msg_W2, 'msg_b2': msg_b2, 'upd_W1': upd_W1, 'upd_b1': upd_b1, 'upd_W2': upd_W2, 'upd_b2': upd_b2, 'ln_gamma': ln_gamma, 'ln_beta': ln_beta}
    _L1_gnn_all = _L1_gnn_setup()
    _L1_gnn_in = {k: v for k, v in _L1_gnn_all.items() if k in ('msg_W1', 'msg_b1', 'msg_W2', 'msg_b2', 'upd_W1', 'upd_b1', 'upd_W2', 'upd_b2', 'ln_gamma', 'ln_beta')}
    del _L1_gnn_all
    return {'x': x, 'src': src, 'dst': dst, 'edge_attr_128': edge_attr_128, 'edge_type_16': edge_type_16, 'L0_gnn_W_rel': _L0_gnn_in['W_rel'], 'L0_gnn_W_root': _L0_gnn_in['W_root'], 'L0_gnn_bias': _L0_gnn_in['bias'], 'L1_gnn_msg_W1': _L1_gnn_in['msg_W1'], 'L1_gnn_msg_b1': _L1_gnn_in['msg_b1'], 'L1_gnn_msg_W2': _L1_gnn_in['msg_W2'], 'L1_gnn_msg_b2': _L1_gnn_in['msg_b2'], 'L1_gnn_upd_W1': _L1_gnn_in['upd_W1'], 'L1_gnn_upd_b1': _L1_gnn_in['upd_b1'], 'L1_gnn_upd_W2': _L1_gnn_in['upd_W2'], 'L1_gnn_upd_b2': _L1_gnn_in['upd_b2'], 'L1_gnn_ln_gamma': _L1_gnn_in['ln_gamma'], 'L1_gnn_ln_beta': _L1_gnn_in['ln_beta']}

def reference(x, src, dst, edge_attr_128, edge_type_16, L0_gnn_W_rel, L0_gnn_W_root, L0_gnn_bias, L1_gnn_msg_W1, L1_gnn_msg_b1, L1_gnn_msg_W2, L1_gnn_msg_b2, L1_gnn_upd_W1, L1_gnn_upd_b1, L1_gnn_upd_W2, L1_gnn_upd_b2, L1_gnn_ln_gamma, L1_gnn_ln_beta):
    import jax
    import jax.numpy as jnp

    def _L0_gnn_ref(node_features, edge_index, edge_type, W_rel, W_root, bias):
        import jax, jax.numpy as jnp
        import numpy as np
        N_NODES = 50000
        N_EDGES = 25000
        D_IN = 128
        D_OUT = 128
        N_REL = 16
        "RGCNConv (PyG semantics, aggr='mean' per relation) + ReLU.\n\n            out[i] = sum_r W_r^T . mean_{j: (j->i, r) in E} x[j] + W_root^T . x[i] + b\n            Dropout is identity in eval mode (reference runs in eval).\n            "
        n_nodes, d_in = node_features.shape
        n_rel = W_rel.shape[0]
        src, dst = (edge_index[0], edge_index[1])
        seg = dst * n_rel + edge_type
        num_segments = n_nodes * n_rel
        ones = jnp.ones(src.shape[0], dtype=node_features.dtype)
        cnt = jax.ops.segment_sum(ones, seg, num_segments=num_segments)
        msg_sum = jax.ops.segment_sum(node_features[src], seg, num_segments=num_segments)
        agg = msg_sum / jnp.maximum(cnt, 1.0)[:, None]
        agg = agg.reshape(n_nodes, n_rel, d_in)
        out = jnp.einsum('nri,rio->no', agg, W_rel)
        out = out + node_features @ W_root + bias
        return jax.nn.relu(out)

    def _L1_gnn_ref(x, edge_index, edge_attr, msg_W1, msg_b1, msg_W2, msg_b2, upd_W1, upd_b1, upd_W2, upd_b2, ln_gamma, ln_beta):
        import jax, jax.numpy as jnp
        import numpy as np
        N_NODES = 50000
        N_EDGES = 10000
        HID = 128
        LN_EPS = 1e-05

        def _layer_norm(h, gamma, beta):
            mu = jnp.mean(h, axis=-1, keepdims=True)
            var = jnp.mean(jnp.square(h - mu), axis=-1, keepdims=True)
            return (h - mu) * jax.lax.rsqrt(var + LN_EPS) * gamma + beta
        src, dst = (edge_index[0], edge_index[1])
        msg_in = jnp.concatenate([x[src], x[dst], edge_attr], axis=-1)
        h = jax.nn.relu(msg_in @ msg_W1 + msg_b1)
        messages = h @ msg_W2 + msg_b2
        aggregated = jax.ops.segment_sum(messages, dst, num_segments=x.shape[0])
        upd_in = jnp.concatenate([x, aggregated], axis=-1)
        u = jax.nn.relu(upd_in @ upd_W1 + upd_b1)
        updated = u @ upd_W2 + upd_b2
        return _layer_norm(x + updated, ln_gamma, ln_beta)
    edge_index = jnp.stack([src, dst])
    x = _layernorm(x + _L0_gnn_ref(x, edge_index, edge_type_16, L0_gnn_W_rel, L0_gnn_W_root, L0_gnn_bias), axis=-1)
    x = _layernorm(x + _L1_gnn_ref(x, edge_index, edge_attr_128, L1_gnn_msg_W1, L1_gnn_msg_b1, L1_gnn_msg_W2, L1_gnn_msg_b2, L1_gnn_upd_W1, L1_gnn_upd_b1, L1_gnn_upd_W2, L1_gnn_upd_b2, L1_gnn_ln_gamma, L1_gnn_ln_beta), axis=-1)
    return x

_drawn_inputs = setup_inputs


def setup_inputs(seed=0):
    import zlib

    import numpy as np

    out = dict(_drawn_inputs(seed))
    spreads = {'L0_gnn_bias': (0.0, 0.1),
     'L1_gnn_msg_b1': (0.0, 0.8),
     'L1_gnn_msg_b2': (0.0, 0.617),
     'L1_gnn_upd_b1': (0.0, 0.1),
     'L1_gnn_upd_b2': (0.0, 0.1),
     'L1_gnn_ln_gamma': (1.0, 0.2),
     'L1_gnn_ln_beta': (0.0, 0.1)}
    factors = {}
    for name, (base, spread) in spreads.items():
        noise = np.random.default_rng([zlib.crc32(name.encode()), seed]).standard_normal(out[name].shape)
        drawn = base * np.exp(spread * noise) if base else spread * noise
        out[name] = jnp.asarray(drawn.astype(out[name].dtype))
    for name, factor in factors.items():
        out[name] = (out[name] * factor).astype(out[name].dtype)
    return out
```

```python
from contextlib import ExitStack

import concourse.bass as bass
from concourse import mybir

P = 128
D = 128
R = 16
BLOCK = 2 * P
GROUP = 4 * P
EPS = 1e-5

ALU = mybir.AluOpType
ACT = mybir.ActivationFunctionType
F32 = mybir.dt.float32
BF16 = mybir.dt.bfloat16
I32 = mybir.dt.int32
AXX = mybir.AxisListType.X


class At:

    def __init__(self, v, c):
        self.v, self.c = v, c
        self.slot = c % 2

    def back(self, k):
        return At(self.v, self.c - k)

    @property
    def n(self):
        return self.v + self.c

    def times(self, per):
        return self.v * (per // 2) + per * (self.c // 2 + 1)

    def within(self, lo, hi):
        return not isinstance(self.v, int) or lo <= self.v + self.c < hi


def build(nc, A, out):
    N, E = A["x"].shape[0], A["src"].shape[0]
    NB = -(-E // BLOCK)
    NB += NB % 2
    NG = -(-N // GROUP)
    assert NG == 2 * NB and E >= BLOCK * (NB - 1)
    LAST_EDGE = E - BLOCK
    LAST_NODE = N - GROUP
    REPEATED = (BLOCK * NB - E) // 2
    NQ = NB // 2
    SEGS = N * R
    DUMP = 2 * BLOCK
    TABLE = -(-(N + DUMP) // GROUP) * GROUP

    ctx = ExitStack()
    with ctx:
        def sb(name, shape, dt=F32):
            return ctx.enter_context(nc.sbuf_tensor(name, shape, dt))

        def sem(name):
            return ctx.enter_context(nc.semaphore(name))

        def sems(name):
            return [sem(f"{name}_slot{i}") for i in range(2)]

        streams = sb("streams", [P, 18, 4 * D])
        taken = [0]

        def rows():
            taken[0] += 2
            return [streams[:, taken[0] - 2 + i, :].rearrange("p (t d) -> p t d", t=4) for i in range(2)]

        def flat(a):
            return a.rearrange("p t d -> p (t d)")

        def dram(name, shape, dt=F32):
            return nc.dram_tensor(name, shape, dt, kind="Internal").ap()

        agg0 = dram("agg0", (TABLE, D))
        agg1 = dram("agg1", (TABLE, D))
        count = dram("count", (SEGS + DUMP, 1))
        xs_kept = dram("xs_kept", (NB * BLOCK, D))
        xd_kept = dram("xd_kept", (NB * BLOCK, D))
        x1d_kept = dram("x1d_kept", (NB * BLOCK, D))
        parts_kept = dram("parts_kept", (3, 3 * D), BF16)

        ident = sb("ident", [P, P])
        earlier = sb("earlier", [P, 2, P])
        zeros = sb("zeros", [P, 4 * D])
        eps = sb("eps", [P, 1])
        w_rel = sb("w_rel", [P, R, D])
        w_root = sb("w_root", [P, D])
        m1 = sb("m1", [P, 3, D])
        m2 = sb("m2", [P, D])
        u1 = sb("u1", [P, 2, D])
        u2 = sb("u2", [P, D])
        u2c = sb("u2c", [P, D])
        m1_b = sb("m1_b", [P, 1])
        u1_b = sb("u1_b", [P, 1])
        gamma = sb("gamma", [P, D])
        beta = sb("beta", [P, D])
        b_row = sb("b_row", [1, 3, D])
        b_parts = sb("b_parts", [1, 3, 3, D], BF16)
        b_back = sb("b_back", [1, 3, D])
        bias = sb("bias", [3, 3, 4, D], BF16)
        ones3 = sb("ones3", [3, P], BF16)
        w_stats = sb("w_stats", [P, 2, 6])
        w_mean = sb("w_mean", [P, 2, 2])

        idx_rows = sb("idx_rows", [NB, 3, BLOCK], I32)
        key_rows = streams[0:NB, 16:18, :].rearrange("b g (q k) -> b (g q) k", q=2)
        SRC, SEG, DST, TYP = 0, 2, 4, 6
        keys = sb("keys", [P, NB, 8])
        I_SRC, I_DSTX, I_SEG, I_DST, I_PUT = 0, 2, 4, 6, 8
        index = sb("index", [P, NB, 10], I32)
        pair = sb("pair", [P, 2], I32)
        pair_f = sb("pair_f", [P, 2])
        dump_i = sb("dump_i", [P, 4], I32)
        dump = sb("dump", [P, 4])

        y_all = sb("y_all", [P, 2 * NB, D])
        key = [sb(f"key{i}", [P, 8]) for i in range(2)]
        idx = [sb(f"idx{i}", [P, 10], I32) for i in range(2)]
        xs = [sb(f"xs{i}", [P, 2, D]) for i in range(2)]
        xd = [sb(f"xd{i}", [P, 2, D]) for i in range(2)]
        xsT = [sb(f"xsT{i}", [P, 2 * P]) for i in range(2)]
        masked = [streams[:, 8 * i:8 * i + 8, :].rearrange("p a (r e) -> p (a r) e", r=2) for i in range(2)]
        same = sb("same", [P, 6, 2 * P], BF16)
        cnt_new = [sb(f"cnt_new{i}", [P, 2]) for i in range(2)]
        dup = sb("dup", [P, 4])
        to_dump = sb("to_dump", [P, 4])
        moved = sb("moved", [P, 4])
        put_cnt = [sb(f"put_cnt{i}", [P, 2], I32) for i in range(2)]
        cnt = [sb(f"cnt{i}", [P, 2]) for i in range(2)]
        inv = sb("inv", [P, 2, 2])

        val = [sb(f"val{i}", [P, 2, D]) for i in range(2)]
        eq = sb("eq", [P, 2, 2 * P])
        put = [sb(f"put{i}", [P, 2, D]) for i in range(2)]
        pkey = [sb(f"pkey{i}", [P, 2]) for i in range(2)]
        pidx = [sb(f"pidx{i}", [P, 2], I32) for i in range(2)]

        dx, ds, dx1, dr, do = (rows() for _ in range(5))
        dt = sb("dt", [P, 4, D])
        dx1b = sb("dx1b", [P, 4, D])
        dq = sb("dq", [P, 4, D])
        dxT = sb("dxT", [P, 4 * P])
        dx1T = sb("dx1T", [P, 4 * P])
        daT = sb("daT", [P, 4 * P])
        duT = [sb(f"duT{i}", [P, 4 * P]) for i in range(2)]
        d_st = sb("d_st", [P, 2, 4, 6])
        d_mv1 = [sb(f"d_mv1{i}", [P, 4, 2]) for i in range(2)]
        d_mv3 = sb("d_mv3", [P, 4, 2])
        d_small = sb("d_small", [P, 9, 4])
        d_junk = sb("d_junk", [P, 4, D], BF16)
        SD1, RS1, NM1, SS2, SD2, RS2, SD3, RS3, NM3 = range(9)

        ex, ea, es, ex1 = (rows() for _ in range(4))
        exT = flat(y_all[:, 4:8, :])
        ex1T = flat(y_all[:, 8:12, :])
        attr = [y_all[:, 12 + 2 * i:14 + 2 * i, :] for i in range(2)]
        attrT = flat(y_all[:, 16:18, :])
        hT = [flat(y_all[:, 18 + 2 * i:20 + 2 * i, :]) for i in range(2)]
        e_st = sb("e_st", [P, 4, 6])
        e_mv = [sb(f"e_mv{i}", [P, 4, 2]) for i in range(2)]
        e_small = sb("e_small", [P, 2, 4])
        qidx = [sb(f"qidx{i}", [P, 2, 10], I32) for i in range(2)]
        oidx = [sb(f"oidx{i}", [P, 2, 2], I32) for i in range(2)]

        bank = [ctx.enter_context(nc.psum_tensor(f"bank{i}", [P, 4 * P], F32)) for i in range(8)]
        dT_ps, dY_ps, dU_ps, dV_ps, eT_ps, eY_ps, eH_ps, eM_ps = bank
        keys_ps = bank[0:2]
        typ_ps = bank[2:4]
        y_ps = bank[4:6]

        load_i = sem("load_i")
        load_r = sem("load_r")
        load_w = sem("load_w")
        load_b = sem("load_b")
        load_p = sem("load_p")
        parts_out = sem("parts_out")
        c_pool = sem("c_pool")
        c_dve = sem("c_dve")
        c_key = sem("c_key")
        c_keyT = sem("c_keyT")
        c_cols = sem("c_cols")
        c_zero = sem("c_zero")
        passed = sem("passed")
        c_parts = sem("c_parts")
        c_weights = sem("c_weights")
        zeroed_c = sem("zeroed_c")
        zeroed0 = sem("zeroed0")
        zeroed1 = sem("zeroed1")
        a_staged = sem("a_staged")
        a_src, a_dst = sems("a_src"), sems("a_dst")
        a_kept_s, a_kept_d = sems("a_kept_s"), sems("a_kept_d")
        a_keys_ps = sem("a_keys_ps")
        a_xsT_ps = sem("a_xsT_ps")
        a_xsT = sem("a_xsT")
        a_masked = sem("a_masked")
        a_y_ps = sem("a_y_ps")
        a_y = sem("a_y")
        a_same = sem("a_same")
        a_dup = sem("a_dup")
        a_put = sem("a_put")
        a_counted = sem("a_counted")
        b_staged = sem("b_staged")
        b_cnt = sems("b_cnt")
        b_max = sem("b_max")
        b_inv = sem("b_inv")
        s_staged = sem("s_staged")
        s_val = sem("s_val")
        s_keys_ps = sem("s_keys_ps")
        s_eq = sem("s_eq")
        s_sum_ps = sem("s_sum_ps")
        s_sum = sem("s_sum")
        s_added = sem("s_added")
        d_x = sems("d_x")
        d_xT_ps, d_xT, d_y_ps, d_s, d_stats1, d_mv1s = (sem(f"d_{n}") for n in ("xT_ps", "xT", "y_ps", "s", "stats1", "mv1s"))
        d_sd1, d_rs1, d_nm1, d_x1, d_x1T_ps, d_x1T = (sem(f"d_{n}") for n in ("sd1", "rs1", "nm1", "x1", "x1T_ps", "x1T"))
        d_u_ps, d_uT, d_v_ps, d_t, d_ss2, d_sd2, d_rs2 = (sem(f"d_{n}") for n in ("u_ps", "uT", "v_ps", "t", "ss2", "sd2", "rs2"))
        d_x1b, d_qg, d_nm3 = sem("d_x1b"), sem("d_qg"), sem("d_nm3")
        d_r, d_stats3, d_mv3s, d_sd3, d_rs3, d_o = (sem(f"d_{n}") for n in ("r", "stats3", "mv3s", "sd3", "rs3", "o"))
        d_stored = sems("d_stored")
        e_staged = sem("e_staged")
        e_x, e_agg, e_attr = sems("e_x"), sems("e_agg"), sems("e_attr")
        e_xT_ps, e_xT, e_y_ps, e_v, e_s, e_stats, e_mvs = (sem(f"e_{n}") for n in ("xT_ps", "xT", "y_ps", "v", "s", "stats", "mvs"))
        e_sd, e_rs, e_x1, e_x1T_ps, e_x1T = (sem(f"e_{n}") for n in ("sd", "rs", "x1", "x1T_ps", "x1T"))
        e_attrT_ps, e_attrT, e_h_ps, e_hT, e_m_ps = (sem(f"e_{n}") for n in ("attrT_ps", "attrT", "h_ps", "hT", "m_ps"))
        e_kept = sems("e_kept")
        q_staged = sem("q_staged")
        o_staged = sem("o_staged")
        q_x1, q_agg = sems("q_x1"), sems("q_agg")
        q_aT_ps, q_aT = sem("q_aT_ps"), sem("q_aT")
        q_out = sem("q_out")

        def after(eng, s, n):
            if not isinstance(n, int) or n > 0:
                eng.wait_ge(s, n)

        def apart(eng):
            eng.sem_inc(passed, 1)

        def each(eng, stop, peel_first, peel_last, step):
            lo, hi = peel_first, (stop - peel_last) // 2 * 2
            if hi - lo < 4:
                lo = hi = stop
            for n in range(lo):
                step(At(0, n))
            if hi > lo:
                with eng.Fori(lo // 2, hi // 2) as turn:
                    step(At(turn * 2, 0))
                    step(At(turn * 2, 1))
            for n in range(hi, stop):
                step(At(0, n))

        COUNT_PARTS = [(at, min(4 * D, (SEGS + DUMP - at) // P)) for at in range(0, SEGS + DUMP, 4 * D * P)]
        assert (SEGS + DUMP) % P == 0

        def flat_rows(a):
            return a[:, :, :].rearrange("p t d -> p (t d)")

        def wide(small):
            return small.unsqueeze(2).to_broadcast([P, 4, D])

        def bank4(ps):
            return ps[:, :].rearrange("p (t d) -> p t d", t=4)

        def edge_rows(table, b):
            return table.rearrange("(b p j) d -> b p (j d)", p=P, j=2)[b]

        block = ctx.enter_context(nc.Block())

        @block.sync
        def _(sp):
            full = BLOCK * (NB - 1)
            for q, name in enumerate(("src", "dst", "edge_type_16")):
                a = A[name]
                sp.dma_start(idx_rows[0:NB - 1, q, :], a[0:full].rearrange("(b k) -> b k", k=BLOCK)).then_inc(load_i, 16)
                sp.dma_start(idx_rows[NB - 1:NB, q, :], a[LAST_EDGE:E].rearrange("(b k) -> b k", k=BLOCK)).then_inc(load_i, 16)
            sp.dma_start(w_rel[:, :, :], A["L0_gnn_W_rel"].rearrange("r i o -> i r o")).then_inc(load_r, 16)
            for q, name in enumerate(("L0_gnn_bias", "L1_gnn_msg_b2", "L1_gnn_upd_b2")):
                sp.dma_start(b_row[0:1, q, :], A[name].rearrange("(a n) -> a n", a=1)).then_inc(load_b, 16)
            sp.wait_ge(c_zero, 1)
            flat = count.rearrange("n a -> (n a)")
            for at, cols in COUNT_PARTS:
                sp.dma_start(flat[at:at + P * cols].rearrange("(p c) -> p c", p=P), zeros[:, 0:cols]).then_inc(zeroed_c, 16)
            for dst, src in ((w_root[:, :], A["L0_gnn_W_root"]),
                             (m1[:, :, :], A["L1_gnn_msg_W1"].rearrange("(k i) o -> i k o", k=3)),
                             (m2[:, :], A["L1_gnn_msg_W2"]),
                             (u1[:, :, :], A["L1_gnn_upd_W1"].rearrange("(k i) o -> i k o", k=2)),
                             (u2[:, :], A["L1_gnn_upd_W2"]),
                             (m1_b[:, :], A["L1_gnn_msg_b1"].rearrange("(n a) -> n a", a=1)),
                             (u1_b[:, :], A["L1_gnn_upd_b1"].rearrange("(n a) -> n a", a=1)),
                             (gamma[:, :], A["L1_gnn_ln_gamma"].rearrange("(a n) -> a n", a=1).to_broadcast([P, D])),
                             (beta[:, :], A["L1_gnn_ln_beta"].rearrange("(a n) -> a n", a=1).to_broadcast([P, D]))):
                sp.dma_start(dst, src).then_inc(load_w, 16)
            def zero_rows(i):
                for table, s in ((agg0, zeroed0), (agg1, zeroed1)):
                    sp.dma_start(table.rearrange("(g p r) d -> g p (r d)", p=P, r=4)[i], zeros[:, :]).then_inc(s, 16)

            def keep_rows(b):
                sp.wait_ge(a_src[b.slot], b.times(32))
                sp.dma_start(edge_rows(xs_kept, b.n), flat_rows(xs[b.slot])).then_inc(a_kept_s[b.slot], 16)
                sp.wait_ge(a_dst[b.slot], b.times(32))
                sp.dma_start(edge_rows(xd_kept, b.n), flat_rows(xd[b.slot])).then_inc(a_kept_d[b.slot], 16)
                zero_rows(b.n * 2)
                zero_rows(b.n * 2 + 1)

            each(sp, NB, 0, 0, keep_rows)
            for i in range(2 * NB, TABLE // GROUP):
                zero_rows(i)

            def load_nodes(g):
                if not g.within(0, NG):
                    return
                after(sp, d_xT_ps, g.n - 1)
                after(sp, d_s, g.n - 1)
                if isinstance(g.v, int) and g.n == NG - 1:
                    src = A["x"][LAST_NODE:N].rearrange("(p r) d -> p (r d)", r=4)
                else:
                    src = A["x"][0:(NG - 1) * GROUP].rearrange("(g p r) d -> g p (r d)", p=P, r=4)[g.n]
                sp.dma_start(flat_rows(dx[g.slot]), src).then_inc(d_x[g.slot], 16)

            def store_nodes(g):
                if not g.within(0, NG):
                    return
                after(sp, d_o, g.n + 1)
                if isinstance(g.v, int) and g.n == NG - 1:
                    sp.wait_ge(d_stored[g.back(1).slot], g.back(1).times(16))
                    dst = out[LAST_NODE:N].rearrange("(p r) d -> p (r d)", r=4)
                else:
                    dst = out[0:(NG - 1) * GROUP].rearrange("(g p r) d -> g p (r d)", p=P, r=4)[g.n]
                sp.dma_start(dst, flat_rows(do[g.slot])).then_inc(d_stored[g.slot], 16)

            def phase2(b):
                load_nodes(b.back(-1))
                store_nodes(b.back(3))

            sp.wait_ge(c_parts, 1)
            sp.dma_start(parts_kept.rearrange("(a k) n -> a (k n)", a=1),
                         b_parts[:, :, :, :].rearrange("a k q n -> a (k q n)")).then_inc(parts_out, 16)
            sp.wait_ge(parts_out, 16)
            for t in range(4):
                sp.dma_start(bias[:, :, t, :], parts_kept.rearrange("k (q n) -> k q n", q=3)).then_inc(load_p, 16)

            sp.wait_ge(a_y_ps, NB)
            load_nodes(At(0, 0))
            each(sp, NB, 6, 0, phase2)

            def load_ends(b):
                if not b.within(0, NB):
                    return
                after(sp, e_xT_ps, b.n - 1)
                after(sp, e_s, b.n - 1)
                e = flat_rows(ex[b.slot])
                sp.dma_start(e[:, 0:2 * D], edge_rows(xs_kept, b.n)).then_inc(e_x[b.slot], 16)
                sp.dma_start(e[:, 2 * D:4 * D], edge_rows(xd_kept, b.n)).then_inc(e_x[b.slot], 16)

            def load_attr(b):
                if not b.within(0, NB):
                    return
                after(sp, e_attrT_ps, b.n - 1)
                if isinstance(b.v, int) and b.n == NB - 1:
                    src = A["edge_attr_128"][LAST_EDGE:E].rearrange("(p j) d -> p (j d)", j=2)
                else:
                    src = edge_rows(A["edge_attr_128"][0:full], b.n)
                sp.dma_start(flat_rows(attr[b.slot]), src).then_inc(e_attr[b.slot], 16)

            def keep_x1(b):
                if not b.within(0, NB):
                    return
                sp.wait_ge(e_x1, b.n + 1)
                sp.dma_start(edge_rows(x1d_kept, b.n), flat_rows(ex1[b.slot])[:, 2 * D:4 * D]).then_inc(e_kept[b.slot], 16)

            def phase3(b):
                i = b.back(-NB)
                load_nodes(i.back(-1))
                keep_x1(b.back(2))
                load_ends(b.back(-1))
                load_attr(b.back(1))
                store_nodes(i.back(3))

            sp.wait_ge(s_val, NB)
            for s in range(2):
                sp.wait_ge(a_kept_s[s], 16 * (NB // 2))
                sp.wait_ge(a_kept_d[s], 16 * (NB // 2))
            load_ends(At(0, 0))
            each(sp, NB + 3, 6, 5, phase3)

            def load_x1(q):
                g = q.back(-NG)
                sp.wait_ge(d_r, g.n - 1)
                src = x1d_kept.rearrange("(q b p j) d -> q p b (j d)", b=2, p=P, j=2)[q.n]
                dst = dx1[g.slot].rearrange("p (b j) d -> p b (j d)", j=2)
                sp.dma_start(dst, src).then_inc(q_x1[g.slot], 16)

            for s in range(2):
                sp.wait_ge(e_kept[s], 16 * (NB // 2))
            each(sp, NQ, 0, 0, load_x1)
            for s in range(2):
                sp.wait_ge(d_stored[s], 16 * (NG // 2))

        @block.gpsimd
        def _(pool):
            pool.memset(zeros[:, :], 0.0).then_inc(c_zero, 1)
            pool.memset(ident[:, :], 0.0).then_inc(c_pool, 1)
            pool.memset(earlier[:, :, :], 1.0).then_inc(c_pool, 1)
            pool.memset(ones3[:, :], 1.0)
            pool.memset(eps[:, :], EPS)
            pool.iota(pair[:, :], pattern=[[1, 2]], base=0, channel_multiplier=2)
            pool.iota(dump_i[:, 0:2], pattern=[[P, 2]], base=SEGS + BLOCK, channel_multiplier=1)
            pool.iota(dump_i[:, 2:4], pattern=[[P, 2]], base=N + BLOCK, channel_multiplier=1).then_inc(c_pool, 1)
            pool.wait_ge(c_pool, 3)
            pool.affine_select(out=ident[:, :], in_=ident[:, :], compare_op=ALU.not_equal, fill=1.0, base=0,
                               pattern=[[-1, P]], channel_multiplier=1).then_inc(c_pool, 1)
            pool.affine_select(out=earlier[:, 1, :], in_=earlier[:, 1, :], compare_op=ALU.is_gt, fill=0.0, base=0,
                               pattern=[[-1, P]], channel_multiplier=1).then_inc(c_pool, 1)

            def gather(dst, table, at, s):
                pool.indirect_dma_start(dst, None, table, bass.IndirectOffsetOnAxis(at, 0)).then_inc(s, 16)

            def add_rows(table, at, src, s):
                pool.indirect_dma_start(table, bass.IndirectOffsetOnAxis(at, 0), src, None,
                                        compute_op=ALU.add).then_inc(s, 16)

            def gather_x(b):
                if not b.within(0, NB):
                    return
                pool.wait_ge(a_staged, b.n + 1)
                if b.back(2).within(0, NB):
                    pool.wait_ge(a_kept_s[b.slot], b.back(2).times(16))
                    pool.wait_ge(a_kept_d[b.slot], b.back(2).times(16))
                    pool.wait_ge(a_xsT_ps, b.n - 1)
                apart(pool)
                for j in range(2):
                    gather(xs[b.slot][:, j, :], A["x"], idx[b.slot][:, I_SRC + j:I_SRC + j + 1], a_src[b.slot])
                for j in range(2):
                    gather(xd[b.slot][:, j, :], A["x"], idx[b.slot][:, I_DSTX + j:I_DSTX + j + 1], a_dst[b.slot])

            def add_counts(b):
                if not b.within(0, NB):
                    return
                pool.wait_ge(a_put, b.n + 1)
                after(pool, a_counted, b.n * 32)
                apart(pool)
                for j in range(2):
                    add_rows(count, put_cnt[b.slot][:, j:j + 1], cnt_new[b.slot][:, j:j + 1], a_counted)

            def phase1(b):
                gather_x(b.back(-2))
                add_counts(b)

            pool.wait_ge(zeroed_c, 16 * len(COUNT_PARTS))
            gather_x(At(0, 0))
            gather_x(At(0, 1))
            each(pool, NB, 4, 2, phase1)

            def gather_counts(b):
                if not b.within(0, NB):
                    return
                pool.wait_ge(b_staged, b.n + 1)
                after(pool, b_inv, b.n - 1)
                apart(pool)
                for j in range(2):
                    gather(cnt[b.slot][:, j:j + 1], count, idx[b.slot][:, I_SEG + j:I_SEG + j + 1], b_cnt[b.slot])

            def add_sums(n, table, valid):
                if not valid:
                    return
                pool.wait_ge(s_sum, n.n + 1)
                after(pool, s_added, n.n * 32)
                apart(pool)
                for j in range(2):
                    add_rows(table, pidx[n.slot][:, j:j + 1], put[n.slot][:, j, :], s_added)

            def d_beta(g, last=NG):
                if not g.within(0, last):
                    return
                if last == NG:
                    pool.wait_ge(d_x1, g.n + 1)
                else:
                    pool.wait_ge(q_x1[g.slot], g.back(NG).times(16))
                after(pool, d_r, g.n)
                pool.tensor_tensor(dx1b[:, :, :], dx1[g.slot], beta[:, :].unsqueeze(1).to_broadcast([P, 4, D]),
                                   ALU.add).then_inc(d_x1b, 1)

            def phase2(b):
                gather_counts(b.back(1))
                add_sums(b.back(2), agg0, b.back(2).within(0, NB))
                if b.within(0, NB):
                    d_beta(b.back(2))

            pool.wait_ge(a_counted, 32 * NB)
            pool.wait_ge(zeroed0, 16 * (TABLE // GROUP))
            each(pool, NB + 2, 6, 2, phase2)

            def gather_agg0(b):
                if not b.within(0, NB):
                    return
                pool.wait_ge(e_staged, b.n + 1)
                after(pool, e_v, b.n - 1)
                apart(pool)
                for t, c in enumerate((I_SRC, I_SRC + 1, I_DST, I_DST + 1)):
                    gather(ea[b.slot][:, t, :], agg0, idx[b.slot][:, c:c + 1], e_agg[b.slot])

            def phase3(b):
                i = b.back(-NB)
                gather_agg0(b)
                d_beta(i.back(2))
                add_sums(i.back(3), agg1, b.back(3).within(0, NB))

            pool.wait_ge(s_added, 32 * NB)
            pool.wait_ge(zeroed1, 16 * (TABLE // GROUP))
            each(pool, NB + 3, 6, 5, phase3)

            def gather_agg1(q, blk):
                for j in range(2):
                    gather(ea[q.slot][:, 2 * blk + j, :], agg1, qidx[q.slot][:, blk, I_DST + j:I_DST + j + 1], q_agg[q.slot])

            def scatter_out(q, blk):
                after(pool, q_out, q.n * 64 + 32 * blk)
                apart(pool)
                for j in range(2):
                    pool.indirect_dma_start(out, bass.IndirectOffsetOnAxis(oidx[q.slot][:, blk, j:j + 1], 0),
                                            do[q.slot][:, 2 * blk + j, :], None,
                                            bounds_check=N - 1, oob_is_err=False).then_inc(q_out, 16)

            def phase4(k):
                gathers, scatters = k.within(0, NQ), k.back(3).within(0, NQ)
                q = k.back(3)
                if scatters:
                    pool.wait_ge(d_o, q.n + NG + 1)
                    pool.wait_ge(o_staged, q.n + 1)
                    scatter_out(q, 0)
                if gathers:
                    pool.wait_ge(q_staged, k.n + 1)
                    after(pool, q_aT_ps, k.n - 1)
                    apart(pool)
                    gather_agg1(k, 0)
                if k.back(2).within(0, NQ):
                    d_beta(k.back(2).back(-NG), NG + NQ)
                if scatters:
                    scatter_out(q, 1)
                if gathers:
                    gather_agg1(k, 1)

            pool.wait_ge(s_added, 64 * NB)
            for s in range(2):
                pool.wait_ge(d_stored[s], 16 * (NG // 2))
            each(pool, NQ + 3, 6, 3, phase4)
            pool.wait_ge(q_out, 64 * NQ)

        @block.tensor
        def _(pe):
            def transpose(ps, rows_, n=P):
                return pe.transpose(ps, rows_, ident[0:n, 0:n])

            pe.wait_ge(c_pool, 5)
            pe.wait_ge(c_key, 1)
            for q in range(4):
                for j in range(2):
                    at = (2 * (q % 2) + j) * NB
                    mm = transpose(bank[q // 2][:, at:at + NB], key_rows[:, q, j:BLOCK:2], NB)
            mm.then_inc(c_keyT, 1)

            def key_and_x(b):
                if not b.within(0, NB):
                    return
                pe.wait_ge(a_staged, b.n + 1)
                after(pe, a_put, b.n - 1)
                k = key[b.slot]
                for t in range(4):
                    transpose(keys_ps[b.slot][:, t * P:t * P + P], k[:, SEG + t:SEG + t + 1].to_broadcast([P, P]))
                for t in range(2):
                    mm = transpose(typ_ps[b.slot][:, t * P:t * P + P], k[:, TYP + t:TYP + t + 1].to_broadcast([P, P]))
                mm.then_inc(a_keys_ps, 1)
                pe.wait_ge(a_src[b.slot], b.times(32))
                after(pe, a_xsT, b.n - 1)
                for j in range(2):
                    mm = transpose(typ_ps[b.slot][:, (2 + j) * P:(3 + j) * P], xs[b.slot][:, j, :])
                mm.then_inc(a_xsT_ps, 1)

            def by_type(b):
                if not b.within(0, NB):
                    return
                after(pe, a_y, b.n - 1)
                for j in range(2):
                    for r in range(R):
                        if j == 0 and r % 4 == 0:
                            pe.wait_ge(a_masked, (b.n * (R // 4)) + r // 4 + 1)
                        mm = pe.matmul(y_ps[b.slot][:, j * D:j * D + D], masked[b.slot][:, r, j * P:j * P + P],
                                       w_rel[:, r, :], start=(r == 0), stop=(r == R - 1))
                mm.then_inc(a_y_ps, 1)

            def phase1(b):
                by_type(b.back(1))
                key_and_x(b.back(-1))

            pe.wait_ge(c_cols, 1)
            pe.wait_ge(load_r, 16)
            key_and_x(At(0, 0))
            each(pe, NB + 1, 4, 3, phase1)

            def sum_keys(n, valid):
                if not valid:
                    return
                pe.wait_ge(s_staged, n.n + 1)
                after(pe, s_eq, n.n)
                after(pe, s_val, n.n)
                for i in range(2):
                    mm = transpose(eM_ps[:, (2 + i) * P:(3 + i) * P], pkey[n.slot][:, i:i + 1].to_broadcast([P, P]))
                mm.then_inc(s_keys_ps, 1)

            def sum_same(n, valid):
                if not valid:
                    return
                pe.wait_ge(s_eq, n.n + 1)
                pe.wait_ge(s_val, n.n + 1)
                after(pe, s_sum, n.n)
                for i in range(2):
                    for j in range(2):
                        mm = pe.matmul(eH_ps[:, (2 + i) * P:(3 + i) * P], eq[:, j, i * P:i * P + P],
                                       val[n.slot][:, j, :], start=(j == 0), stop=(j == 1))
                mm.then_inc(s_sum_ps, 1)

            def d_transpose_x(g):
                if not g.within(0, NG):
                    return
                pe.wait_ge(d_x[g.slot], g.times(16))
                after(pe, d_x1T, g.n - 1)
                for t in range(4):
                    mm = transpose(dT_ps[:, t * P:t * P + P], dx[g.slot][:, t, :])
                mm.then_inc(d_xT_ps, 1)

            def d_root(g):
                if not g.within(0, NG):
                    return
                pe.wait_ge(d_xT, g.n + 1)
                after(pe, d_s, g.n)
                for t in range(4):
                    pe.matmul(dY_ps[:, t * D:t * D + D], dxT[:, t * P:t * P + P], w_root[:, :],
                                   start=(t == 0), stop=False, skip_group_check=True)
                mm = pe.matmul(dY_ps[:, :], ones3[:, :], bias[:, 0, :, :].rearrange("k t d -> k (t d)"), start=False, stop=True,
                               skip_group_check=True)
                mm.then_inc(d_y_ps, 1)

            def d_transpose_x1(g):
                if not g.within(0, NG):
                    return
                pe.wait_ge(d_x1, g.n + 1)
                pe.wait_ge(d_xT, g.n + 2 if g.back(-1).within(0, NG) else g.n + 1)
                for t in range(4):
                    mm = transpose(dT_ps[:, t * P:t * P + P], dx1[g.slot][:, t, :])
                mm.then_inc(d_x1T_ps, 1)

            def d_update1(g, last=NG, agg=False):
                if not g.within(0, last):
                    return
                pe.wait_ge(d_x1T, g.n + 1)
                after(pe, d_uT, g.n)
                mm = pe.matmul(dU_ps[:, :], u1[:, 0, :], dx1T[:, :], start=True, stop=not agg)
                if agg:
                    pe.wait_ge(q_aT, g.n - NG + 1)
                    mm = pe.matmul(dU_ps[:, :], u1[:, 1, :], daT[:, :], start=False, stop=True)
                mm.then_inc(d_u_ps, 1)

            def d_update2(g, last=NG):
                if not g.within(0, last):
                    return
                pe.wait_ge(d_uT, g.n + 1)
                after(pe, d_t, g.n)
                for t in range(4):
                    pe.matmul(dV_ps[:, t * D:t * D + D], duT[g.slot][:, t * P:t * P + P], u2c[:, :],
                                   start=(t == 0), stop=False, skip_group_check=True)
                mm = pe.matmul(dV_ps[:, :], ones3[:, :], bias[:, 2, :, :].rearrange("k t d -> k (t d)"), start=False, stop=True,
                               skip_group_check=True)
                mm.then_inc(d_v_ps, 1)

            def phase2(b):
                n = b.back(1)
                dense = b.within(0, NB)
                if dense:
                    d_transpose_x(b)
                    d_root(b)
                    d_transpose_x1(b.back(1))
                sum_keys(n, n.within(0, NB))
                if dense:
                    d_update1(b.back(1))
                sum_same(n, n.within(0, NB))
                if dense:
                    d_update2(b.back(1))

            pe.wait_ge(load_w, 16 * 9)
            pe.wait_ge(load_p, 16 * 4)
            pe.wait_ge(c_weights, 1)
            each(pe, NB + 1, 6, 1, phase2)

            def e_transpose_x(b):
                if not b.within(0, NB):
                    return
                pe.wait_ge(e_x[b.slot], b.times(32))
                after(pe, e_attrT, b.n - 1)
                for t in range(4):
                    mm = transpose(eT_ps[:, t * P:t * P + P], ex[b.slot][:, t, :])
                mm.then_inc(e_xT_ps, 1)

            def e_root(b):
                if not b.within(0, NB):
                    return
                pe.wait_ge(e_xT, b.n + 1)
                after(pe, e_v, b.n)
                for t in range(4):
                    pe.matmul(eY_ps[:, t * D:t * D + D], exT[:, t * P:t * P + P], w_root[:, :],
                                   start=(t == 0), stop=False, skip_group_check=True)
                mm = pe.matmul(eY_ps[:, :], ones3[:, :], bias[:, 0, :, :].rearrange("k t d -> k (t d)"), start=False, stop=True,
                               skip_group_check=True)
                mm.then_inc(e_y_ps, 1)

            def e_transpose_x1(b):
                if not b.within(0, NB):
                    return
                pe.wait_ge(e_x1, b.n + 1)
                pe.wait_ge(e_xT, b.n + 2 if b.back(-1).within(0, NB) else b.n + 1)
                for t in range(4):
                    mm = transpose(eT_ps[:, t * P:t * P + P], ex1[b.slot][:, t, :])
                mm.then_inc(e_x1T_ps, 1)

            def e_transpose_attr(b):
                if not b.within(0, NB):
                    return
                pe.wait_ge(e_attr[b.slot], b.times(16))
                pe.wait_ge(e_x1T, b.n + 1)
                for t in range(2):
                    mm = transpose(eT_ps[:, t * P:t * P + P], attr[b.slot][:, t, :])
                mm.then_inc(e_attrT_ps, 1)

            def e_message1(b):
                if not b.within(0, NB):
                    return
                pe.wait_ge(e_attrT, b.n + 1)
                after(pe, e_hT, b.n)
                pe.wait_ge(s_sum, b.n + NB)
                pe.matmul(eH_ps[:, 0:2 * P], m1[:, 0, :], ex1T[:, 0:2 * P], start=True, stop=False)
                pe.matmul(eH_ps[:, 0:2 * P], m1[:, 1, :], ex1T[:, 2 * P:4 * P], start=False, stop=False)
                pe.matmul(eH_ps[:, 0:2 * P], m1[:, 2, :], attrT[:, :], start=False, stop=True).then_inc(e_h_ps, 1)

            def e_message2(b):
                if not b.within(0, NB):
                    return
                pe.wait_ge(e_hT, b.n + 1)
                pe.wait_ge(s_eq, b.n + NB + 1)
                for t in range(2):
                    pe.matmul(eM_ps[:, t * D:t * D + D], hT[b.slot][:, t * P:t * P + P], m2[:, :],
                                   start=(t == 0), stop=False, skip_group_check=True)
                mm = pe.matmul(eM_ps[:, 0:2 * D], ones3[:, :], bias[:, 1, 0:2, :].rearrange("k t d -> k (t d)"), start=False, stop=True,
                               skip_group_check=True)
                mm.then_inc(e_m_ps, 1)

            def phase3(b):
                i = b.back(-NB)
                m = b.back(2)
                n, valid = m.back(-NB), m.within(0, NB)
                d_transpose_x(i)
                e_transpose_attr(m)
                e_message2(b.back(3))
                d_root(i)
                e_transpose_x(b)
                d_transpose_x1(i.back(1))
                sum_same(n.back(1), b.back(3).within(0, NB))
                e_root(b)
                d_update1(i.back(1))
                sum_keys(n, valid)
                e_message1(m)
                e_transpose_x1(b.back(1))
                d_update2(i.back(1))

            each(pe, NB + 3, 6, 5, phase3)

            def q_transposes(q):
                if not q.within(0, NQ):
                    return
                g = q.back(-NG)
                pe.wait_ge(q_x1[g.slot], q.times(16))
                pe.wait_ge(d_x1T, g.n)
                for t in range(4):
                    mm = transpose(dT_ps[:, t * P:t * P + P], dx1[g.slot][:, t, :])
                mm.then_inc(d_x1T_ps, 1)
                pe.wait_ge(q_agg[q.slot], q.times(64))
                after(pe, q_aT, q.n)
                for t in range(4):
                    mm = transpose(eT_ps[:, t * P:t * P + P], ea[q.slot][:, t, :])
                mm.then_inc(q_aT_ps, 1)

            def phase4(k):
                q_transposes(k.back(1))
                if k.back(2).within(0, NQ):
                    d_update2(k.back(2).back(-NG), NG + NQ)
                if k.back(1).within(0, NQ):
                    d_update1(k.back(1).back(-NG), NG + NQ, True)

            each(pe, NQ + 2, 6, 2, phase4)

        @block.scalar
        def _(act):
            def copy(dst, src):
                return act.activation(dst, src, ACT.Copy)

            def copy_xsT(b):
                if not b.within(0, NB):
                    return
                act.wait_ge(a_xsT_ps, b.n + 1)
                after(act, a_masked, (b.n - 1) * (R // 4))
                copy(xsT[b.slot][:, :], typ_ps[b.slot][:, 2 * P:4 * P]).then_inc(a_xsT, 1)

            def copy_y(b):
                if not b.within(0, NB):
                    return
                act.wait_ge(a_y_ps, b.n + 1)
                copy(y_all[:, bass.ds(b.n * 2, 2), :].rearrange("p t d -> p (t d)"), y_ps[b.slot][:, 0:2 * D]).then_inc(a_y, 1)

            def phase1(b):
                copy_y(b.back(1))
                copy_xsT(b.back(-1))

            act.wait_ge(c_pool, 5)
            copy_xsT(At(0, 0))
            each(act, NB + 1, 4, 3, phase1)

            def copy_sum(n, valid):
                if not valid:
                    return
                act.wait_ge(s_sum_ps, n.n + 1)
                after(act, s_added, (n.n - 1) * 32)
                copy(flat_rows(put[n.slot]), eH_ps[:, 2 * P:4 * P]).then_inc(s_sum, 1)

            def d_root1(g):
                if not g.within(0, NG):
                    return
                act.wait_ge(d_mv1s, g.n + 1)
                after(act, d_rs1, g.n)
                act.activation(d_small[:, SD1, :], d_mv1[g.slot][:, :, 1], ACT.Sqrt, bias=eps[:, 0:1]).then_inc(d_sd1, 1)

            def d_norm1(g):
                if not g.within(0, NG):
                    return
                act.wait_ge(d_nm1, g.n + 1)
                after(act, d_x1b, g.n - 1)
                after(act, d_t, g.n - 1)
                after(act, d_x1T_ps, g.n - 1)
                for t in range(4):
                    ins = act.activation(dx1[g.slot][:, t, :], ds[g.slot][:, t, :], ACT.Identity,
                                         bias=d_small[:, NM1, t:t + 1], scale=d_small[:, RS1, t:t + 1])
                ins.then_inc(d_x1, 1)

            def d_copy_xT(g):
                if not g.within(0, NG):
                    return
                act.wait_ge(d_xT_ps, g.n + 1)
                after(act, d_y_ps, g.n)
                copy(dxT[:, :], dT_ps[:, :]).then_inc(d_xT, 1)

            def d_copy_x1T(g, last=NG):
                if not g.within(0, last):
                    return
                act.wait_ge(d_x1T_ps, g.n + 1)
                after(act, d_u_ps, g.n)
                copy(dx1T[:, :], dT_ps[:, :]).then_inc(d_x1T, 1)

            def d_relu(g, last=NG):
                if not g.within(0, last):
                    return
                act.wait_ge(d_u_ps, g.n + 1)
                after(act, d_v_ps, g.n - 1)
                act.activation(duT[g.slot][:, :], dU_ps[:, :], ACT.Relu, bias=u1_b[:, 0:1]).then_inc(d_uT, 1)

            def d_root2(g, last=NG):
                if not g.within(0, last):
                    return
                act.wait_ge(d_t, g.n + 1)
                after(act, d_sd2, g.n)
                for t in range(4):
                    ins = act.activation(d_junk[:, t, :], dt[:, t, :], ACT.Square, accum_out=d_small[:, SS2, t:t + 1])
                ins.then_inc(d_ss2, 1)
                act.wait_ge(d_ss2, g.n + 1)
                after(act, d_rs2, g.n)
                act.activation(d_small[:, SD2, :], d_small[:, SS2, :], ACT.Sqrt, bias=eps[:, 0:1], scale=1.0 / D).then_inc(d_sd2, 1)

            def d_root3(g, last=NG):
                if not g.within(0, last):
                    return
                act.wait_ge(d_mv3s, g.n + 1)
                after(act, d_rs3, g.n)
                act.activation(d_small[:, SD3, :], d_mv3[:, :, 1], ACT.Sqrt, bias=eps[:, 0:1]).then_inc(d_sd3, 1)

            def d_norm3(g, last=NG):
                if not g.within(0, last):
                    return
                act.wait_ge(d_nm3, g.n + 1)
                if last == NG:
                    if g.back(2).within(0, last):
                        act.wait_ge(d_stored[g.slot], g.back(2).times(16))
                else:
                    after(act, q_out, (g.n - NG - 1) * 64)
                for t in range(4):
                    ins = act.activation(do[g.slot][:, t, :], dr[g.slot][:, t, :], ACT.Identity,
                                         bias=d_small[:, NM3, t:t + 1], scale=d_small[:, RS3, t:t + 1])
                ins.then_inc(d_o, 1)

            def phase2(b):
                n = b.back(1)
                if b.within(0, NB):
                    d_copy_xT(b)
                    d_norm1(b.back(1))
                    d_copy_x1T(b.back(1))
                    d_root2(b.back(2))
                    d_root3(b.back(3))
                    d_relu(b.back(1))
                copy_sum(n, n.within(0, NB))
                if b.within(0, NB):
                    d_root1(b)
                    d_norm3(b.back(3))

            each(act, NB + 1, 6, 1, phase2)

            def e_root(b):
                if not b.within(0, NB):
                    return
                act.wait_ge(e_mvs, b.n + 1)
                after(act, e_rs, b.n)
                act.activation(e_small[:, 0, :], e_mv[b.slot][:, :, 1], ACT.Sqrt, bias=eps[:, 0:1]).then_inc(e_sd, 1)

            def e_copy_xT(b):
                if not b.within(0, NB):
                    return
                act.wait_ge(e_xT_ps, b.n + 1)
                after(act, e_y_ps, b.n)
                copy(exT[:, :], eT_ps[:, :]).then_inc(e_xT, 1)

            def e_copy_message(b):
                if not b.within(0, NB):
                    return
                act.wait_ge(e_m_ps, b.n + 1)
                after(act, s_sum_ps, b.n + NB - 1)
                copy(flat_rows(val[b.slot]), eM_ps[:, 0:2 * D]).then_inc(s_val, 1)

            def e_copy_x1T(b):
                if not b.within(0, NB):
                    return
                act.wait_ge(e_x1T_ps, b.n + 1)
                after(act, e_h_ps, b.n)
                copy(ex1T[:, :], eT_ps[:, :]).then_inc(e_x1T, 1)

            def e_copy_attrT(b):
                if not b.within(0, NB):
                    return
                act.wait_ge(e_attrT_ps, b.n + 1)
                copy(attrT[:, :], eT_ps[:, 0:2 * P]).then_inc(e_attrT, 1)

            def e_relu(b):
                if not b.within(0, NB):
                    return
                act.wait_ge(e_h_ps, b.n + 1)
                after(act, e_m_ps, b.n - 1)
                act.activation(hT[b.slot][:, :], eH_ps[:, 0:2 * P], ACT.Relu, bias=m1_b[:, 0:1]).then_inc(e_hT, 1)

            def phase3(b):
                i = b.back(-NB)
                m = b.back(3)
                d_copy_xT(i)
                e_copy_attrT(b.back(2))
                d_norm1(i.back(1))
                e_copy_message(m)
                e_copy_xT(b)
                d_root2(i.back(2))
                d_copy_x1T(i.back(1))
                e_root(b.back(1))
                d_root3(i.back(3))
                copy_sum(m.back(-NB), m.within(0, NB))
                d_relu(i.back(1))
                d_root1(i)
                e_relu(b.back(2))
                e_copy_x1T(b.back(1))
                d_norm3(i.back(3))

            each(act, NB + 3, 6, 5, phase3)

            def phase4(k):
                g = k.back(-NG)
                last = NG + NQ
                if k.back(3).within(0, NQ):
                    d_root3(g.back(3), last)
                if k.back(2).within(0, NQ):
                    d_relu(g.back(2), last)
                if k.back(3).within(0, NQ):
                    d_norm3(g.back(3), last)
                if k.back(1).within(0, NQ):
                    d_copy_x1T(g.back(1), last)
                if k.back(2).within(0, NQ):
                    d_root2(g.back(2), last)
                if k.back(1).within(0, NQ):
                    act.wait_ge(q_aT_ps, k.n)
                    after(act, d_u_ps, g.n - 1)
                    copy(daT[:, :], eT_ps[:, :]).then_inc(q_aT, 1)

            for s in range(2):
                act.wait_ge(d_stored[s], 16 * (NG // 2))
            each(act, NQ + 3, 6, 3, phase4)

        @block.vector
        def _(dve):
            tt, stt, ts, cp = dve.tensor_tensor, dve.scalar_tensor_tensor, dve.tensor_scalar, dve.tensor_copy
            chain = [0]

            def link(ins):
                chain[0] += 1
                ins.then_inc(c_dve, 1)
                dve.wait_ge(c_dve, chain[0])

            dve.wait_ge(load_i, 16 * 6)
            for q, row in ((0, 0), (1, 2), (2, 3)):
                ins = cp(key_rows[:, row, :], idx_rows[:, q, :])
            link(ins)
            stt(out=key_rows[:, 1, :], in0=key_rows[:, 2, :], scalar=float(R), in1=key_rows[:, 3, :],
                op0=ALU.mult, op1=ALU.add).then_inc(c_key, 1)
            dve.wait_ge(c_keyT, 1)
            for h in range(2):
                ins = cp(keys[:, :, 4 * h:4 * h + 4].rearrange("p b k -> p k b"),
                         bank[h][:, 0:4 * NB].rearrange("p (k b) -> p k b", b=NB))
            ins.then_inc(c_cols, 1)
            dve.wait_ge(c_cols, 1)
            dve.wait_ge(c_pool, 5)
            cp(pair_f[:, :], pair[:, :])
            link(cp(dump[:, :], dump_i[:, :]))
            if REPEATED:
                ts(keys[0:REPEATED, NB - 1, SEG:SEG + 2], pair_f[0:REPEATED, :], float(SEGS), None, ALU.add)
                link(ts(keys[0:REPEATED, NB - 1, DST:DST + 2], pair_f[0:REPEATED, :], float(N), None, ALU.add))
            cp(index[:, :, I_SRC:I_SRC + 2], keys[:, :, SRC:SRC + 2])
            ts(index[:, :, I_DSTX:I_DSTX + 2], keys[:, :, DST:DST + 2], float(N - 1), None, ALU.min)
            link(cp(index[:, :, I_SEG:I_SEG + 4], keys[:, :, SEG:SEG + 4]))

            def stage1(b):
                if not b.within(0, NB):
                    return
                if b.back(2).within(0, NB):
                    dve.wait_ge(a_put, b.n - 1)
                    dve.wait_ge(a_src[b.slot], b.back(2).times(32))
                    dve.wait_ge(a_dst[b.slot], b.back(2).times(32))
                cp(key[b.slot][:, :], keys[:, b.n, :])
                cp(idx[b.slot][:, 0:4], index[:, b.n, 0:4]).then_inc(a_staged, 1)

            def mask(b):
                dve.wait_ge(a_keys_ps, b.n + 1)
                dve.wait_ge(a_xsT, b.n + 1)
                after(dve, a_y_ps, b.n - 1)
                for r in range(R):
                    ins = stt(out=masked[b.slot][:, r, :], in0=typ_ps[b.slot][:, 0:2 * P], scalar=float(r),
                              in1=xsT[b.slot][:, :], op0=ALU.is_equal, op1=ALU.mult)
                    if r % 4 == 3:
                        ins.then_inc(a_masked, 1)

            def count_same(b):
                k, ps, c = key[b.slot], keys_ps[b.slot], cnt_new[b.slot]
                after(dve, a_counted, (b.n - 1) * 32)
                after(dve, a_put, b.n)
                for j in range(2):
                    ts(same[:, j, :], ps[:, 0:2 * P], k[:, SEG + j:SEG + j + 1], 0.0, ALU.is_equal, ALU.add,
                       accum_out=c[:, j:j + 1])
                for w, at in ((0, SEG), (1, DST)):
                    stt(out=same[:, 2 + 2 * w, 0:P], in0=ps[:, 2 * w * P:(2 * w + 1) * P], scalar=k[:, at:at + 1],
                        in1=earlier[:, 1, :], op0=ALU.is_equal, op1=ALU.mult, accum_out=dup[:, 2 * w:2 * w + 1])
                    stt(out=same[:, 3 + 2 * w, :], in0=ps[:, 2 * w * P:(2 * w + 2) * P], scalar=k[:, at + 1:at + 2],
                        in1=earlier[:, :, :].rearrange("p i k -> p (i k)"), op0=ALU.is_equal, op1=ALU.mult,
                        accum_out=dup[:, 2 * w + 1:2 * w + 2])
                stt(out=to_dump[:, :], in0=k[:, SEG:SEG + 4], scalar=-1.0, in1=dump[:, :],
                    op0=ALU.mult, op1=ALU.add).then_inc(a_same, 1)
                dve.wait_ge(a_same, b.n + 1)
                stt(out=moved[:, :], in0=dup[:, :], scalar=0.0, in1=to_dump[:, :],
                    op0=ALU.is_gt, op1=ALU.mult).then_inc(a_dup, 1)
                dve.wait_ge(a_dup, b.n + 1)
                tt(put_cnt[b.slot][:, :], moved[:, 0:2], k[:, SEG:SEG + 2], ALU.add)
                tt(index[:, b.n, I_PUT:I_PUT + 2], moved[:, 2:4], k[:, DST:DST + 2], ALU.add).then_inc(a_put, 1)

            def phase1(b):
                mask(b)
                count_same(b)
                stage1(b.back(-2))

            stage1(At(0, 0))
            stage1(At(0, 1))
            each(dve, NB, 4, 2, phase1)

            def stage_sum(n, b, valid):
                if not valid:
                    return
                after(dve, s_eq, n.n - 1)
                after(dve, s_added, (n.n - 1) * 32)
                cp(pkey[n.slot][:, :], keys[:, b.n, DST:DST + 2])
                cp(pidx[n.slot][:, :], index[:, b.n, I_PUT:I_PUT + 2]).then_inc(s_staged, 1)

            def equal(n, valid):
                if not valid:
                    return
                dve.wait_ge(s_keys_ps, n.n + 1)
                after(dve, s_sum_ps, n.n)
                for j in range(2):
                    ins = ts(eq[:, j, :], eM_ps[:, 2 * P:4 * P], pkey[n.slot][:, j:j + 1], None, ALU.is_equal)
                ins.then_inc(s_eq, 1)

            def stage2(b):
                if not b.within(0, NB):
                    return
                if b.back(2).within(0, NB):
                    dve.wait_ge(b_cnt[b.slot], b.back(2).times(32))
                cp(idx[b.slot][:, I_SEG:I_SEG + 2], index[:, b.n, I_SEG:I_SEG + 2]).then_inc(b_staged, 1)

            def invert(b):
                if not b.within(0, NB):
                    return
                dve.wait_ge(b_cnt[b.slot], b.times(32))
                after(dve, s_val, b.n)
                ts(inv[:, 0, :], cnt[b.slot][:, :], 1.0, None, ALU.max).then_inc(b_max, 1)
                dve.wait_ge(b_max, b.n + 1)
                dve.reciprocal(inv[:, 1, :], inv[:, 0, :]).then_inc(b_inv, 1)

            def weigh(b):
                if not b.within(0, NB):
                    return
                dve.wait_ge(b_inv, b.n + 1)
                after(dve, s_sum_ps, b.n - 1)
                tt(val[b.slot][:, :, :], y_all[:, bass.ds(b.n * 2, 2), :],
                   inv[:, 1, :].unsqueeze(2).to_broadcast([P, 2, D]), ALU.mult).then_inc(s_val, 1)

            def d_scale1(g):
                if not g.within(0, NG):
                    return
                dve.wait_ge(d_sd1, g.n + 1)
                after(dve, d_x1, g.n)
                dve.reciprocal(d_small[:, RS1, :], d_small[:, SD1, :]).then_inc(d_rs1, 1)
                dve.wait_ge(d_rs1, g.n + 1)
                stt(out=d_small[:, NM1, :], in0=d_mv1[g.slot][:, :, 0], scalar=-1.0, in1=d_small[:, RS1, :],
                    op0=ALU.mult, op1=ALU.mult).then_inc(d_nm1, 1)

            def d_sum(g):
                if not g.within(0, NG):
                    return
                dve.wait_ge(d_y_ps, g.n + 1)
                after(dve, d_x1, g.n - 1)
                stt(out=ds[g.slot], in0=bank4(dY_ps), scalar=0.0, in1=dx[g.slot], op0=ALU.max, op1=ALU.add).then_inc(d_s, 1)

            def d_bn1(g):
                if not g.within(0, NG):
                    return
                dve.wait_ge(d_s, g.n + 1)
                after(dve, d_mv1s, g.n)
                for t in range(4):
                    ins = dve.bn_stats(d_st[:, 0, t, :], ds[g.slot][:, t, :])
                ins.then_inc(d_stats1, 1)

            def d_aggr1(g):
                if not g.within(0, NG):
                    return
                dve.wait_ge(d_stats1, g.n + 1)
                after(dve, d_nm1, g.n - 1)
                apart(dve)
                for t in range(4):
                    ins = dve.bn_aggr(d_mv1[g.slot][:, t, :], d_st[:, 0, t, :])
                ins.then_inc(d_mv1s, 1)

            def d_add2(g, last=NG):
                if not g.within(0, last):
                    return
                dve.wait_ge(d_v_ps, g.n + 1)
                after(dve, d_qg, g.n)
                tt(dt[:, :, :], bank4(dV_ps), dx1[g.slot], ALU.add).then_inc(d_t, 1)

            def d_scale2(g, last=NG):
                if not g.within(0, last):
                    return
                dve.wait_ge(d_sd2, g.n + 1)
                after(dve, d_qg, g.n)
                dve.reciprocal(d_small[:, RS2, :], d_small[:, SD2, :]).then_inc(d_rs2, 1)

            def d_gamma(g, last=NG):
                if not g.within(0, last):
                    return
                dve.wait_ge(d_rs2, g.n + 1)
                after(dve, d_r, g.n)
                for t in range(4):
                    ins = stt(out=dq[:, t, :], in0=dt[:, t, :], scalar=d_small[:, RS2, t:t + 1], in1=gamma[:, :],
                              op0=ALU.mult, op1=ALU.mult)
                ins.then_inc(d_qg, 1)

            def d_residual(g, last=NG):
                if not g.within(0, last):
                    return
                dve.wait_ge(d_qg, g.n + 1)
                dve.wait_ge(d_x1b, g.n + 1)
                after(dve, d_o, g.n - 1)
                tt(dr[g.slot], dq[:, :, :], dx1b[:, :, :], ALU.add).then_inc(d_r, 1)

            def d_bn3(g, last=NG):
                if not g.within(0, last):
                    return
                dve.wait_ge(d_r, g.n + 1)
                after(dve, d_mv3s, g.n)
                for t in range(4):
                    ins = dve.bn_stats(d_st[:, 1, t, :], dr[g.slot][:, t, :])
                ins.then_inc(d_stats3, 1)

            def d_aggr3(g, last=NG):
                if not g.within(0, last):
                    return
                dve.wait_ge(d_stats3, g.n + 1)
                after(dve, d_nm3, g.n)
                apart(dve)
                for t in range(4):
                    ins = dve.bn_aggr(d_mv3[:, t, :], d_st[:, 1, t, :])
                ins.then_inc(d_mv3s, 1)

            def d_scale3(g, last=NG):
                if not g.within(0, last):
                    return
                dve.wait_ge(d_sd3, g.n + 1)
                after(dve, d_o, g.n)
                dve.reciprocal(d_small[:, RS3, :], d_small[:, SD3, :]).then_inc(d_rs3, 1)
                dve.wait_ge(d_rs3, g.n + 1)
                stt(out=d_small[:, NM3, :], in0=d_mv3[:, :, 0], scalar=-1.0, in1=d_small[:, RS3, :],
                    op0=ALU.mult, op1=ALU.mult).then_inc(d_nm3, 1)

            def phase2(b):
                n = b.back(1)
                valid, dense = n.within(0, NB), b.within(0, NB)
                if dense:
                    d_gamma(b.back(3))
                stage2(b)
                stage_sum(n, n, valid)
                if dense:
                    d_residual(b.back(3))
                    d_scale1(b.back(1))
                    d_bn3(b.back(3))
                invert(n)
                if dense:
                    d_add2(b.back(2))
                    d_aggr3(b.back(3))
                    d_sum(b)
                weigh(n)
                if dense:
                    d_bn1(b)
                equal(n, valid)
                if dense:
                    d_aggr1(b)
                    d_scale2(b.back(2))
                    d_scale3(b.back(3))

            dve.wait_ge(load_w, 16 * 9)
            dve.wait_ge(load_b, 16 * 3)
            dve.bn_stats(w_stats[:, 0, :], u2[:, :])
            link(dve.bn_stats(w_stats[0:1, 1, :], b_row[:, 2, :]))
            dve.bn_aggr(w_mean[:, 0, :], w_stats[:, 0, :])
            link(dve.bn_aggr(w_mean[0:1, 1, :], w_stats[0:1, 1, :]))
            ts(u2c[:, :], u2[:, :], w_mean[:, 0, 0:1], None, ALU.subtract).then_inc(c_weights, 1)
            link(ts(b_row[:, 2, :], b_row[:, 2, :], w_mean[0:1, 1, 0:1], None, ALU.subtract))
            for k in range(3):
                link(cp(b_parts[:, k, :, :], b_row[:, :, :]))
                if k < 2:
                    link(cp(b_back[:, :, :], b_parts[:, k, :, :]))
                    link(tt(b_row[:, :, :], b_row[:, :, :], b_back[:, :, :], ALU.subtract))
            dve.engine_nop().then_inc(c_parts, 1)

            dve.wait_ge(a_put, NB)
            dve.wait_ge(a_src[0], 16 * NB)
            dve.wait_ge(a_src[1], 16 * NB)
            dve.wait_ge(a_dst[0], 16 * NB)
            dve.wait_ge(a_dst[1], 16 * NB)
            dve.wait_ge(a_y, NB)
            each(dve, NB + 1, 6, 1, phase2)

            def stage3(b):
                if not b.within(0, NB):
                    return
                if b.back(2).within(0, NB):
                    dve.wait_ge(e_agg[b.slot], b.back(2).times(64))
                cp(idx[b.slot][:, :], index[:, b.n, :]).then_inc(e_staged, 1)

            def e_scale(b):
                if not b.within(0, NB):
                    return
                dve.wait_ge(e_sd, b.n + 1)
                after(dve, e_x1, b.n)
                dve.reciprocal(e_small[:, 1, :], e_small[:, 0, :]).then_inc(e_rs, 1)

            def e_norm(b):
                if not b.within(0, NB):
                    return
                dve.wait_ge(e_rs, b.n + 1)
                if b.back(2).within(0, NB):
                    dve.wait_ge(e_kept[b.slot], b.back(2).times(16))
                    dve.wait_ge(e_x1T_ps, b.n - 1)
                for t in range(4):
                    ins = ts(ex1[b.slot][:, t, :], es[b.slot][:, t, :], e_mv[b.slot][:, t, 0:1], e_small[:, 1, t:t + 1],
                             ALU.subtract, ALU.mult)
                ins.then_inc(e_x1, 1)

            def e_add(b):
                if not b.within(0, NB):
                    return
                dve.wait_ge(e_y_ps, b.n + 1)
                dve.wait_ge(e_agg[b.slot], b.times(64))
                after(dve, e_x1, b.n - 1)
                tt(es[b.slot], bank4(eY_ps), ea[b.slot], ALU.add).then_inc(e_v, 1)

            def e_sum(b):
                if not b.within(0, NB):
                    return
                dve.wait_ge(e_v, b.n + 1)
                stt(out=es[b.slot], in0=es[b.slot], scalar=0.0, in1=ex[b.slot], op0=ALU.max, op1=ALU.add).then_inc(e_s, 1)

            def e_bn(b):
                if not b.within(0, NB):
                    return
                dve.wait_ge(e_s, b.n + 1)
                after(dve, e_mvs, b.n)
                for t in range(4):
                    ins = dve.bn_stats(e_st[:, t, :], es[b.slot][:, t, :])
                ins.then_inc(e_stats, 1)

            def e_aggr(b):
                if not b.within(0, NB):
                    return
                dve.wait_ge(e_stats, b.n + 1)
                after(dve, e_x1, b.n - 1)
                apart(dve)
                for t in range(4):
                    ins = dve.bn_aggr(e_mv[b.slot][:, t, :], e_st[:, t, :])
                ins.then_inc(e_mvs, 1)

            def phase3(b):
                i = b.back(-NB)
                m = b.back(2)
                d_gamma(i.back(3))
                equal(i.back(3), b.back(3).within(0, NB))
                d_residual(i.back(3))
                d_scale1(i.back(1))
                d_add2(i.back(2))
                e_bn(b.back(1))
                d_sum(i)
                stage_sum(m.back(-NB), m, m.within(0, NB))
                e_aggr(b.back(1))
                d_bn3(i.back(3))
                d_bn1(i)
                d_aggr3(i.back(3))
                d_aggr1(i)
                stage3(b.back(-1))
                e_scale(b.back(1))
                e_add(b)
                e_norm(b.back(1))
                d_scale2(i.back(2))
                d_scale3(i.back(3))
                e_sum(b)

            for s in range(2):
                dve.wait_ge(b_cnt[s], 16 * NB)
            stage3(At(0, 0))
            each(dve, NB + 3, 6, 5, phase3)

            def stage4(q):
                if not q.within(0, NQ):
                    return
                if q.back(2).within(0, NQ):
                    dve.wait_ge(q_agg[q.slot], q.back(2).times(64))
                cp(qidx[q.slot][:, :, :], index[:, bass.ds(q.n * 2, 2), :]).then_inc(q_staged, 1)

            def stage_out(q):
                if not q.within(0, NQ):
                    return
                after(dve, q_out, (q.n - 1) * 64)
                cp(oidx[q.slot][:, :, :], index[:, bass.ds(q.n * 2, 2), I_PUT:I_PUT + 2]).then_inc(o_staged, 1)

            def phase4(k):
                g = k.back(-NG)
                last = NG + NQ
                stage4(k)
                if k.back(3).within(0, NQ):
                    d_gamma(g.back(3), last)
                    d_residual(g.back(3), last)
                    stage_out(k.back(3))
                    d_bn3(g.back(3), last)
                    d_aggr3(g.back(3), last)
                    d_scale3(g.back(3), last)
                if k.back(2).within(0, NQ):
                    d_add2(g.back(2), last)
                    d_scale2(g.back(2), last)

            each(dve, NQ + 3, 6, 3, phase4)


_INS = ["x", "src", "dst", "edge_attr_128", "edge_type_16", "L0_gnn_W_rel", "L0_gnn_W_root", "L0_gnn_bias",
        "L1_gnn_msg_W1", "L1_gnn_msg_b1", "L1_gnn_msg_W2", "L1_gnn_msg_b2", "L1_gnn_upd_W1", "L1_gnn_upd_b1",
        "L1_gnn_upd_W2", "L1_gnn_upd_b2", "L1_gnn_ln_gamma", "L1_gnn_ln_beta"]


def kernel(**inputs):
    import numpy as _np
    import concourse.bacc as _bacc
    from concourse import mybir as _mybir
    from concourse.bass_utils import run_bass_kernel_spmd as _run

    nc = _bacc.Bacc("TRN2", target_bir_lowering=False, num_devices=1)
    arrays, aps = {}, {}
    for name in _INS:
        a = _np.ascontiguousarray(inputs[name])
        arrays[f"in_{name}"] = a
        aps[name] = nc.dram_tensor(f"in_{name}", a.shape, _mybir.dt.from_np(a.dtype), kind="ExternalInput").ap()
    out = nc.dram_tensor("out_0", arrays["in_x"].shape, _mybir.dt.float32, kind="ExternalOutput").ap()
    build(nc, aps, out)
    r = _run(nc, [arrays], core_ids=[0])
    return r.results[0]["out_0"]
```

```python
from contextlib import ExitStack

import concourse.bass as bass
from concourse import mybir

P = 128
D = 128
R = 16
BLOCK = 2 * P
GROUP = 4 * P
EPS = 1e-5

ALU = mybir.AluOpType
ACT = mybir.ActivationFunctionType
F32 = mybir.dt.float32
BF16 = mybir.dt.bfloat16
I32 = mybir.dt.int32
AXX = mybir.AxisListType.X


class At:

    def __init__(self, v, c):
        self.v, self.c = v, c
        self.slot = c % 2

    def back(self, k):
        return At(self.v, self.c - k)

    @property
    def n(self):
        return self.v + self.c

    def times(self, per):
        return self.v * (per // 2) + per * (self.c // 2 + 1)

    def within(self, lo, hi):
        return not isinstance(self.v, int) or lo <= self.v + self.c < hi


def build(nc, A, out):
    N, E = A["x"].shape[0], A["src"].shape[0]
    NB = -(-E // BLOCK)
    NB += NB % 2
    NG = -(-N // GROUP)
    assert NG == 2 * NB and E >= BLOCK * (NB - 1)
    LAST_EDGE = E - BLOCK
    LAST_NODE = N - GROUP
    REPEATED = (BLOCK * NB - E) // 2
    NQ = NB // 2
    SEGS = N * R
    DUMP = 2 * BLOCK
    TABLE = -(-(N + DUMP) // GROUP) * GROUP

    ctx = ExitStack()
    with ctx:
        def sb(name, shape, dt=F32):
            return ctx.enter_context(nc.sbuf_tensor(name, shape, dt))

        def sem(name):
            return ctx.enter_context(nc.semaphore(name))

        def sems(name):
            return [sem(f"{name}_slot{i}") for i in range(2)]

        streams = sb("streams", [P, 18, 4 * D])
        taken = [0]

        def rows():
            taken[0] += 2
            return [streams[:, taken[0] - 2 + i, :].rearrange("p (t d) -> p t d", t=4) for i in range(2)]

        def flat(a):
            return a.rearrange("p t d -> p (t d)")

        def dram(name, shape, dt=F32):
            return nc.dram_tensor(name, shape, dt, kind="Internal").ap()

        agg0 = dram("agg0", (TABLE, D))
        agg1 = dram("agg1", (TABLE, D))
        count = dram("count", (SEGS + DUMP, 1))
        xs_kept = dram("xs_kept", (NB * BLOCK, D))
        xd_kept = dram("xd_kept", (NB * BLOCK, D))
        x1d_kept = dram("x1d_kept", (NB * BLOCK, D))
        parts_kept = dram("parts_kept", (3, 3 * D), BF16)

        ident = sb("ident", [P, P])
        earlier = sb("earlier", [P, 2, P])
        zeros = sb("zeros", [P, 4 * D])
        eps = sb("eps", [P, 1])
        one = sb("one", [P, 1])
        w_rel = sb("w_rel", [P, R, D])
        w_root = sb("w_root", [P, D])
        m1 = sb("m1", [P, 3, D])
        m2 = sb("m2", [P, D])
        u1 = sb("u1", [P, 2, D])
        u2 = sb("u2", [P, D])
        u2c = sb("u2c", [P, D])
        m1_b = sb("m1_b", [P, 1])
        u1_b = sb("u1_b", [P, 1])
        gamma = sb("gamma", [P, D])
        beta = sb("beta", [P, D])
        b_row = sb("b_row", [1, 3, D])
        b_parts = sb("b_parts", [1, 3, 3, D], BF16)
        b_back = sb("b_back", [1, 3, D])
        bias = sb("bias", [3, 3, 4, D], BF16)
        ones3 = sb("ones3", [3, P], BF16)
        w_stats = sb("w_stats", [P, 2, 6])
        w_mean = sb("w_mean", [P, 2, 2])

        idx_rows = sb("idx_rows", [NB, 3, BLOCK], I32)
        key_rows = streams[0:NB, 16:18, :].rearrange("b g (q k) -> b (g q) k", q=2)
        SRC, SEG, DST, TYP = 0, 2, 4, 6
        keys = sb("keys", [P, NB, 8])
        I_SRC, I_DSTX, I_SEG, I_DST, I_PUT = 0, 2, 4, 6, 8
        index = sb("index", [P, NB, 10], I32)
        pair = sb("pair", [P, 2], I32)
        pair_f = sb("pair_f", [P, 2])
        dump_i = sb("dump_i", [P, 4], I32)
        dump = sb("dump", [P, 4])

        y_all = sb("y_all", [P, 2 * NB, D])
        key = [sb(f"key{i}", [P, 8]) for i in range(2)]
        idx = [sb(f"idx{i}", [P, 10], I32) for i in range(2)]
        xs = [sb(f"xs{i}", [P, 2, D]) for i in range(2)]
        xd = [sb(f"xd{i}", [P, 2, D]) for i in range(2)]
        key_cols = [streams[:, 16 + i, :] for i in range(2)]
        cols = [sb(f"cols{i}", [P, 4 * P]) for i in range(2)]
        masked = [streams[:, 8 * i:8 * i + 8, :].rearrange("p a (r e) -> p (a r) e", r=2) for i in range(2)]
        same = sb("same", [P, 6, 2 * P], BF16)
        cnt_new = [sb(f"cnt_new{i}", [P, 2]) for i in range(2)]
        dup = sb("dup", [P, 4])
        to_dump = sb("to_dump", [P, NB, 4])
        moved = sb("moved", [P, 4])
        put_cnt = [sb(f"put_cnt{i}", [P, 2], I32) for i in range(2)]
        cnt = [sb(f"cnt{i}", [P, 2]) for i in range(2)]
        inv = sb("inv", [P, 2, 2])

        val = [sb(f"val{i}", [P, 2, D]) for i in range(2)]
        eq = sb("eq", [P, 2, 2 * P])
        put = [sb(f"put{i}", [P, 2, D]) for i in range(2)]
        pkey = [sb(f"pkey{i}", [P, 2]) for i in range(2)]
        pidx = [sb(f"pidx{i}", [P, 2], I32) for i in range(2)]

        dx, ds, dx1, dr, do = (rows() for _ in range(5))
        dt = sb("dt", [P, 4, D])
        dx1b = sb("dx1b", [P, 4, D])
        dq = sb("dq", [P, 4, D])
        distance = dq[:, :, :].rearrange("p (j h) d -> p j (h d)", j=2)
        dxT = sb("dxT", [P, 4 * P])
        dx1T = sb("dx1T", [P, 4 * P])
        daT = sb("daT", [P, 4 * P])
        duT = [sb(f"duT{i}", [P, 4 * P]) for i in range(2)]
        d_st = sb("d_st", [P, 2, 4, 6])
        d_mv1 = [sb(f"d_mv1{i}", [P, 4, 2]) for i in range(2)]
        d_mv3 = sb("d_mv3", [P, 4, 2])
        d_small = sb("d_small", [P, 9, 4])
        d_junk = sb("d_junk", [P, 4, D], BF16)
        SD1, RS1, NM1, SS2, SD2, RS2, SD3, RS3, NM3 = range(9)

        ex, ea, es, ex1 = (rows() for _ in range(4))
        exT = flat(y_all[:, 4:8, :])
        ex1T = flat(y_all[:, 8:12, :])
        attr = [y_all[:, 12 + 2 * i:14 + 2 * i, :] for i in range(2)]
        attrT = flat(y_all[:, 16:18, :])
        hT = [flat(y_all[:, 18 + 2 * i:20 + 2 * i, :]) for i in range(2)]
        e_st = sb("e_st", [P, 4, 6])
        e_mv = [sb(f"e_mv{i}", [P, 4, 2]) for i in range(2)]
        e_small = sb("e_small", [P, 2, 4])
        qidx = [sb(f"qidx{i}", [P, 2, 10], I32) for i in range(2)]
        oidx = [sb(f"oidx{i}", [P, 4], I32) for i in range(2)]
        okey = [sb(f"okey{i}", [P, 4]) for i in range(2)]
        odup = sb("odup", [P, 2])
        oput = sb("oput", [P, 4])
        omoved = sb("omoved", [P, 2])

        bank = [ctx.enter_context(nc.psum_tensor(f"bank{i}", [P, 4 * P], F32)) for i in range(8)]
        dT_ps, dY_ps, dU_ps, dV_ps, eT_ps, eY_ps, eH_ps, eM_ps = bank
        keys_ps = bank[0:2]
        typ_ps = bank[2:4]
        y_ps = bank[4:6]

        load_i = sem("load_i")
        load_r = sem("load_r")
        load_w = sem("load_w")
        load_b = sem("load_b")
        load_p = sem("load_p")
        parts_out = sem("parts_out")
        c_pool = sem("c_pool")
        c_dve = sem("c_dve")
        c_key = sem("c_key")
        c_keyT = sem("c_keyT")
        c_cols = sem("c_cols")
        c_zero = sem("c_zero")
        passed = sem("passed")
        c_parts = sem("c_parts")
        c_weights = sem("c_weights")
        zeroed_c = sem("zeroed_c")
        zeroed0 = sem("zeroed0")
        zeroed1 = sem("zeroed1")
        a_idx = sem("a_idx")
        a_staged = sem("a_staged")
        a_src, a_dst = sems("a_src"), sems("a_dst")
        a_kept_s, a_kept_d = sems("a_kept_s"), sems("a_kept_d")
        a_keys_ps = sem("a_keys_ps")
        a_xsT_ps = sem("a_xsT_ps")
        a_cols = sem("a_cols")
        a_key_cols = sem("a_key_cols")
        a_masked = sem("a_masked")
        a_y_ps = sem("a_y_ps")
        a_y = sem("a_y")
        a_distance = sem("a_distance")
        a_cnt = sem("a_cnt")
        a_same = sem("a_same")
        a_dup = sem("a_dup")
        a_put = sem("a_put")
        a_counted = sem("a_counted")
        b_staged = sem("b_staged")
        b_cnt = sems("b_cnt")
        b_max = sem("b_max")
        b_inv = sem("b_inv")
        s_staged = sem("s_staged")
        s_val = sem("s_val")
        s_keys_ps = sem("s_keys_ps")
        s_eq = sem("s_eq")
        s_sum_ps = sem("s_sum_ps")
        s_sum = sem("s_sum")
        s_added = sem("s_added")
        d_x = sems("d_x")
        d_xT_ps, d_xT, d_y_ps, d_s, d_stats1, d_mv1s = (sem(f"d_{n}") for n in ("xT_ps", "xT", "y_ps", "s", "stats1", "mv1s"))
        d_sd1, d_rs1, d_nm1, d_x1, d_x1T_ps, d_x1T = (sem(f"d_{n}") for n in ("sd1", "rs1", "nm1", "x1", "x1T_ps", "x1T"))
        d_u_ps, d_uT, d_v_ps, d_t, d_ss2, d_sd2, d_rs2 = (sem(f"d_{n}") for n in ("u_ps", "uT", "v_ps", "t", "ss2", "sd2", "rs2"))
        d_x1b, d_qg, d_nm3 = sem("d_x1b"), sem("d_qg"), sem("d_nm3")
        d_r, d_stats3, d_mv3s, d_sd3, d_rs3, d_o = (sem(f"d_{n}") for n in ("r", "stats3", "mv3s", "sd3", "rs3", "o"))
        d_stored = sems("d_stored")
        e_staged = sem("e_staged")
        e_x, e_agg, e_attr = sems("e_x"), sems("e_agg"), sems("e_attr")
        e_xT_ps, e_xT, e_y_ps, e_v, e_s, e_stats, e_mvs = (sem(f"e_{n}") for n in ("xT_ps", "xT", "y_ps", "v", "s", "stats", "mvs"))
        e_sd, e_rs, e_x1, e_x1T_ps, e_x1T = (sem(f"e_{n}") for n in ("sd", "rs", "x1", "x1T_ps", "x1T"))
        e_attrT_ps, e_attrT, e_h_ps, e_hT, e_m_ps = (sem(f"e_{n}") for n in ("attrT_ps", "attrT", "h_ps", "hT", "m_ps"))
        e_kept = sems("e_kept")
        q_staged = sem("q_staged")
        o_keys = sem("o_keys")
        o_keys_ps = sem("o_keys_ps")
        o_same = sem("o_same")
        o_moved = sem("o_moved")
        o_staged = sem("o_staged")
        q_x1, q_agg = sems("q_x1"), sems("q_agg")
        q_aT_ps, q_aT = sem("q_aT_ps"), sem("q_aT")
        q_out = sem("q_out")

        def after(eng, s, n):
            if not isinstance(n, int) or n > 0:
                eng.wait_ge(s, n)

        def apart(eng):
            eng.sem_inc(passed, 1)

        def each(eng, stop, peel_first, peel_last, step):
            lo, hi = peel_first, (stop - peel_last) // 2 * 2
            if hi - lo < 4:
                lo = hi = stop
            for n in range(lo):
                step(At(0, n))
            if hi > lo:
                with eng.Fori(lo // 2, hi // 2) as turn:
                    step(At(turn * 2, 0))
                    step(At(turn * 2, 1))
            for n in range(hi, stop):
                step(At(0, n))

        COUNT_PARTS = [(at, min(4 * D, (SEGS + DUMP - at) // P)) for at in range(0, SEGS + DUMP, 4 * D * P)]
        assert (SEGS + DUMP) % P == 0

        def flat_rows(a):
            return a[:, :, :].rearrange("p t d -> p (t d)")

        def wide(small):
            return small.unsqueeze(2).to_broadcast([P, 4, D])

        def bank4(ps):
            return ps[:, :].rearrange("p (t d) -> p t d", t=4)

        def edge_rows(table, b):
            return table.rearrange("(b p j) d -> b p (j d)", p=P, j=2)[b]

        block = ctx.enter_context(nc.Block())

        @block.sync
        def _(sp):
            full = BLOCK * (NB - 1)
            for q, name in enumerate(("src", "dst", "edge_type_16")):
                a = A[name]
                sp.dma_start(idx_rows[0:NB - 1, q, :], a[0:full].rearrange("(b k) -> b k", k=BLOCK)).then_inc(load_i, 16)
                sp.dma_start(idx_rows[NB - 1:NB, q, :], a[LAST_EDGE:E].rearrange("(b k) -> b k", k=BLOCK)).then_inc(load_i, 16)
            sp.dma_start(w_rel[:, :, :], A["L0_gnn_W_rel"].rearrange("r i o -> i r o")).then_inc(load_r, 16)
            for q, name in enumerate(("L0_gnn_bias", "L1_gnn_msg_b2", "L1_gnn_upd_b2")):
                sp.dma_start(b_row[0:1, q, :], A[name].rearrange("(a n) -> a n", a=1)).then_inc(load_b, 16)
            sp.wait_ge(c_zero, 1)
            flat = count.rearrange("n a -> (n a)")
            for at, cols in COUNT_PARTS:
                sp.dma_start(flat[at:at + P * cols].rearrange("(p c) -> p c", p=P), zeros[:, 0:cols]).then_inc(zeroed_c, 16)
            for dst, src in ((w_root[:, :], A["L0_gnn_W_root"]),
                             (m1[:, :, :], A["L1_gnn_msg_W1"].rearrange("(k i) o -> i k o", k=3)),
                             (m2[:, :], A["L1_gnn_msg_W2"]),
                             (u1[:, :, :], A["L1_gnn_upd_W1"].rearrange("(k i) o -> i k o", k=2)),
                             (u2[:, :], A["L1_gnn_upd_W2"]),
                             (m1_b[:, :], A["L1_gnn_msg_b1"].rearrange("(n a) -> n a", a=1)),
                             (u1_b[:, :], A["L1_gnn_upd_b1"].rearrange("(n a) -> n a", a=1)),
                             (gamma[:, :], A["L1_gnn_ln_gamma"].rearrange("(a n) -> a n", a=1).to_broadcast([P, D])),
                             (beta[:, :], A["L1_gnn_ln_beta"].rearrange("(a n) -> a n", a=1).to_broadcast([P, D]))):
                sp.dma_start(dst, src).then_inc(load_w, 16)
            def zero_rows(i):
                for table, s in ((agg0, zeroed0), (agg1, zeroed1)):
                    sp.dma_start(table.rearrange("(g p r) d -> g p (r d)", p=P, r=4)[i], zeros[:, :]).then_inc(s, 16)

            def keep_rows(b):
                sp.wait_ge(a_src[b.slot], b.times(32))
                sp.dma_start(edge_rows(xs_kept, b.n), flat_rows(xs[b.slot])).then_inc(a_kept_s[b.slot], 16)
                sp.wait_ge(a_dst[b.slot], b.times(32))
                sp.dma_start(edge_rows(xd_kept, b.n), flat_rows(xd[b.slot])).then_inc(a_kept_d[b.slot], 16)
                zero_rows(b.n * 2)
                zero_rows(b.n * 2 + 1)

            each(sp, NB, 0, 0, keep_rows)
            for i in range(2 * NB, TABLE // GROUP):
                zero_rows(i)

            def load_nodes(g):
                if not g.within(0, NG):
                    return
                after(sp, d_xT_ps, g.n - 1)
                after(sp, d_s, g.n - 1)
                if isinstance(g.v, int) and g.n == NG - 1:
                    src = A["x"][LAST_NODE:N].rearrange("(p r) d -> p (r d)", r=4)
                else:
                    src = A["x"][0:(NG - 1) * GROUP].rearrange("(g p r) d -> g p (r d)", p=P, r=4)[g.n]
                sp.dma_start(flat_rows(dx[g.slot]), src).then_inc(d_x[g.slot], 16)

            def store_nodes(g):
                if not g.within(0, NG):
                    return
                after(sp, d_o, g.n + 1)
                if isinstance(g.v, int) and g.n == NG - 1:
                    sp.wait_ge(d_stored[g.back(1).slot], g.back(1).times(16))
                    dst = out[LAST_NODE:N].rearrange("(p r) d -> p (r d)", r=4)
                else:
                    dst = out[0:(NG - 1) * GROUP].rearrange("(g p r) d -> g p (r d)", p=P, r=4)[g.n]
                sp.dma_start(dst, flat_rows(do[g.slot])).then_inc(d_stored[g.slot], 16)

            def phase2(b):
                load_nodes(b.back(-1))
                store_nodes(b.back(3))

            sp.wait_ge(c_parts, 1)
            sp.dma_start(parts_kept.rearrange("(a k) n -> a (k n)", a=1),
                         b_parts[:, :, :, :].rearrange("a k q n -> a (k q n)")).then_inc(parts_out, 16)
            sp.wait_ge(parts_out, 16)
            for t in range(4):
                sp.dma_start(bias[:, :, t, :], parts_kept.rearrange("k (q n) -> k q n", q=3)).then_inc(load_p, 16)

            sp.wait_ge(a_y_ps, NB)
            load_nodes(At(0, 0))
            each(sp, NB, 6, 0, phase2)

            def load_ends(b):
                if not b.within(0, NB):
                    return
                after(sp, e_xT_ps, b.n - 1)
                after(sp, e_s, b.n - 1)
                e = flat_rows(ex[b.slot])
                sp.dma_start(e[:, 0:2 * D], edge_rows(xs_kept, b.n)).then_inc(e_x[b.slot], 16)
                sp.dma_start(e[:, 2 * D:4 * D], edge_rows(xd_kept, b.n)).then_inc(e_x[b.slot], 16)

            def load_attr(b):
                if not b.within(0, NB):
                    return
                after(sp, e_attrT_ps, b.n - 1)
                if isinstance(b.v, int) and b.n == NB - 1:
                    src = A["edge_attr_128"][LAST_EDGE:E].rearrange("(p j) d -> p (j d)", j=2)
                else:
                    src = edge_rows(A["edge_attr_128"][0:full], b.n)
                sp.dma_start(flat_rows(attr[b.slot]), src).then_inc(e_attr[b.slot], 16)

            def keep_x1(b):
                if not b.within(0, NB):
                    return
                sp.wait_ge(e_x1, b.n + 1)
                sp.dma_start(edge_rows(x1d_kept, b.n), flat_rows(ex1[b.slot])[:, 2 * D:4 * D]).then_inc(e_kept[b.slot], 16)

            def phase3(b):
                i = b.back(-NB)
                load_nodes(i.back(-1))
                keep_x1(b.back(2))
                load_ends(b.back(-1))
                load_attr(b.back(1))
                store_nodes(i.back(3))

            sp.wait_ge(s_val, NB)
            for s in range(2):
                sp.wait_ge(a_kept_s[s], 16 * (NB // 2))
                sp.wait_ge(a_kept_d[s], 16 * (NB // 2))
            load_ends(At(0, 0))
            each(sp, NB + 3, 6, 5, phase3)

            def load_x1(q):
                g = q.back(-NG)
                sp.wait_ge(d_x1b, g.n - 1)
                sp.wait_ge(d_t, g.n - 1)
                src = x1d_kept.rearrange("(q b p j) d -> q p b (j d)", b=2, p=P, j=2)[q.n]
                dst = dx1[g.slot].rearrange("p (b j) d -> p b (j d)", j=2)
                sp.dma_start(dst, src).then_inc(q_x1[g.slot], 16)

            for s in range(2):
                sp.wait_ge(e_kept[s], 16 * (NB // 2))
            each(sp, NQ, 0, 0, load_x1)
            for s in range(2):
                sp.wait_ge(d_stored[s], 16 * (NG // 2))

        @block.gpsimd
        def _(pool):
            pool.memset(zeros[:, :], 0.0).then_inc(c_zero, 1)
            pool.memset(ident[:, :], 0.0).then_inc(c_pool, 1)
            pool.memset(earlier[:, :, :], 1.0).then_inc(c_pool, 1)
            pool.memset(ones3[:, :], 1.0)
            pool.memset(eps[:, :], EPS)
            pool.memset(one[:, :], 1.0)
            pool.iota(pair[:, :], pattern=[[1, 2]], base=0, channel_multiplier=2)
            pool.iota(dump_i[:, 0:2], pattern=[[P, 2]], base=SEGS + BLOCK, channel_multiplier=1)
            pool.iota(dump_i[:, 2:4], pattern=[[P, 2]], base=N + BLOCK, channel_multiplier=1).then_inc(c_pool, 1)
            pool.wait_ge(c_pool, 3)
            pool.affine_select(out=ident[:, :], in_=ident[:, :], compare_op=ALU.not_equal, fill=1.0, base=0,
                               pattern=[[-1, P]], channel_multiplier=1).then_inc(c_pool, 1)
            pool.affine_select(out=earlier[:, 1, :], in_=earlier[:, 1, :], compare_op=ALU.is_gt, fill=0.0, base=0,
                               pattern=[[-1, P]], channel_multiplier=1).then_inc(c_pool, 1)

            def gather(dst, table, at, s):
                pool.indirect_dma_start(dst, None, table, bass.IndirectOffsetOnAxis(at, 0)).then_inc(s, 16)

            def add_rows(table, at, src, s):
                pool.indirect_dma_start(table, bass.IndirectOffsetOnAxis(at, 0), src, None,
                                        compute_op=ALU.add).then_inc(s, 16)

            def gather_x(b):
                if not b.within(0, NB):
                    return
                pool.wait_ge(a_idx, b.n + 1)
                if b.back(2).within(0, NB):
                    pool.wait_ge(a_kept_s[b.slot], b.back(2).times(16))
                    pool.wait_ge(a_kept_d[b.slot], b.back(2).times(16))
                    pool.wait_ge(a_xsT_ps, b.n - 1)
                apart(pool)
                for j in range(2):
                    gather(xs[b.slot][:, j, :], A["x"], idx[b.slot][:, I_SRC + j:I_SRC + j + 1], a_src[b.slot])
                for j in range(2):
                    gather(xd[b.slot][:, j, :], A["x"], idx[b.slot][:, I_DSTX + j:I_DSTX + j + 1], a_dst[b.slot])

            def add_counts(b):
                if not b.within(0, NB):
                    return
                pool.wait_ge(a_put, b.n + 1)
                pool.wait_ge(a_cnt, b.n + 1)
                after(pool, a_counted, b.n * 32)
                apart(pool)
                for j in range(2):
                    add_rows(count, put_cnt[b.slot][:, j:j + 1], cnt_new[b.slot][:, j:j + 1], a_counted)

            def phase1(b):
                gather_x(b.back(-2))
                add_counts(b)

            pool.wait_ge(zeroed_c, 16 * len(COUNT_PARTS))
            gather_x(At(0, 0))
            gather_x(At(0, 1))
            each(pool, NB, 4, 2, phase1)

            def gather_counts(b):
                if not b.within(0, NB):
                    return
                pool.wait_ge(b_staged, b.n + 1)
                after(pool, b_inv, b.n - 1)
                apart(pool)
                for j in range(2):
                    gather(cnt[b.slot][:, j:j + 1], count, idx[b.slot][:, I_SEG + j:I_SEG + j + 1], b_cnt[b.slot])

            def add_sums(n, table, valid):
                if not valid:
                    return
                pool.wait_ge(s_sum, n.n + 1)
                after(pool, s_added, n.n * 32)
                apart(pool)
                for j in range(2):
                    add_rows(table, pidx[n.slot][:, j:j + 1], put[n.slot][:, j, :], s_added)

            def d_beta(g):
                if not g.within(0, NG):
                    return
                pool.wait_ge(d_x1, g.n + 1)
                after(pool, d_r, g.n)
                pool.tensor_tensor(dx1b[:, :, :], dx1[g.slot], beta[:, :].unsqueeze(1).to_broadcast([P, 4, D]),
                                   ALU.add).then_inc(d_x1b, 1)

            def d_residual(g):
                if not g.within(0, NG):
                    return
                pool.wait_ge(d_qg, g.n + 1)
                pool.wait_ge(d_x1b, g.n + 1)
                after(pool, d_o, g.n - 1)
                pool.tensor_tensor(dr[g.slot], dq[:, :, :], dx1b[:, :, :], ALU.add).then_inc(d_r, 1)

            def phase2(b):
                gather_counts(b.back(1))
                if b.within(0, NB):
                    d_residual(b.back(3))
                    d_beta(b.back(2))
                add_sums(b.back(2), agg0, b.back(2).within(0, NB))

            pool.wait_ge(a_counted, 32 * NB)
            pool.wait_ge(zeroed0, 16 * (TABLE // GROUP))
            each(pool, NB + 2, 6, 2, phase2)

            def gather_agg0(b):
                if not b.within(0, NB):
                    return
                pool.wait_ge(e_staged, b.n + 1)
                after(pool, e_v, b.n - 1)
                apart(pool)
                for t, c in enumerate((I_SRC, I_SRC + 1, I_DST, I_DST + 1)):
                    gather(ea[b.slot][:, t, :], agg0, idx[b.slot][:, c:c + 1], e_agg[b.slot])

            def phase3(b):
                i = b.back(-NB)
                gather_agg0(b)
                d_residual(i.back(3))
                d_beta(i.back(2))
                add_sums(i.back(3), agg1, b.back(3).within(0, NB))

            pool.wait_ge(s_added, 32 * NB)
            pool.wait_ge(zeroed1, 16 * (TABLE // GROUP))
            each(pool, NB + 3, 6, 5, phase3)

            def gather_agg1(q, blk):
                for j in range(2):
                    gather(ea[q.slot][:, 2 * blk + j, :], agg1, qidx[q.slot][:, blk, I_DST + j:I_DST + j + 1], q_agg[q.slot])

            def scatter_out(q):
                pool.wait_ge(d_o, q.n + NG + 1)
                pool.wait_ge(o_staged, q.n + 1)
                after(pool, q_out, q.n * 64)
                apart(pool)
                for t in range(4):
                    pool.indirect_dma_start(out, bass.IndirectOffsetOnAxis(oidx[q.slot][:, t:t + 1], 0),
                                            do[q.slot][:, t, :], None,
                                            bounds_check=N - 1, oob_is_err=False).then_inc(q_out, 16)

            def gather_group(q):
                pool.wait_ge(q_staged, q.n + 1)
                after(pool, q_aT_ps, q.n - 1)
                apart(pool)
                gather_agg1(q, 0)
                gather_agg1(q, 1)

            def phase4(k):
                if k.within(0, NQ):
                    gather_group(k)
                if k.back(3).within(0, NQ):
                    scatter_out(k.back(3))

            pool.wait_ge(s_added, 64 * NB)
            for s in range(2):
                pool.wait_ge(d_stored[s], 16 * (NG // 2))
            each(pool, NQ + 3, 6, 3, phase4)
            pool.wait_ge(q_out, 64 * NQ)

        @block.tensor
        def _(pe):
            def transpose(ps, rows_, n=P):
                return pe.transpose(ps, rows_, ident[0:n, 0:n])

            pe.wait_ge(c_pool, 5)
            pe.wait_ge(c_key, 1)
            for q in range(4):
                for j in range(2):
                    at = (2 * (q % 2) + j) * NB
                    mm = transpose(bank[q // 2][:, at:at + NB], key_rows[:, q, j:BLOCK:2], NB)
            mm.then_inc(c_keyT, 1)

            def key_and_x(b):
                if not b.within(0, NB):
                    return
                pe.wait_ge(a_staged, b.n + 1)
                after(pe, a_key_cols, b.n - 1)
                after(pe, a_cols, b.n - 1)
                k = key[b.slot]
                for t in range(4):
                    mm = transpose(keys_ps[b.slot][:, t * P:t * P + P], k[:, SEG + t:SEG + t + 1].to_broadcast([P, P]))
                mm.then_inc(a_keys_ps, 1)
                for t in range(2):
                    transpose(typ_ps[b.slot][:, t * P:t * P + P], k[:, TYP + t:TYP + t + 1].to_broadcast([P, P]))
                pe.wait_ge(a_src[b.slot], b.times(32))
                for j in range(2):
                    mm = transpose(typ_ps[b.slot][:, (2 + j) * P:(3 + j) * P], xs[b.slot][:, j, :])
                mm.then_inc(a_xsT_ps, 1)

            def by_type(b, j):
                if not b.within(0, NB):
                    return
                after(pe, a_y, b.n - 1)
                for r in range(R):
                    if j == 0 and r % 4 == 0:
                        pe.wait_ge(a_masked, (b.n * (R // 4)) + r // 4 + 1)
                    mm = pe.matmul(y_ps[b.slot][:, j * D:j * D + D], masked[b.slot][:, r, j * P:j * P + P],
                                   w_rel[:, r, :], start=(r == 0), stop=(r == R - 1))
                if j == 1:
                    mm.then_inc(a_y_ps, 1)

            def phase1(b):
                by_type(b.back(1), 0)
                key_and_x(b.back(-1))
                by_type(b.back(1), 1)

            pe.wait_ge(c_cols, 1)
            pe.wait_ge(load_r, 16)
            key_and_x(At(0, 0))
            each(pe, NB + 1, 4, 3, phase1)

            def sum_keys(n, valid):
                if not valid:
                    return
                pe.wait_ge(s_staged, n.n + 1)
                after(pe, s_eq, n.n)
                after(pe, s_val, n.n)
                for i in range(2):
                    mm = transpose(eM_ps[:, (2 + i) * P:(3 + i) * P], pkey[n.slot][:, i:i + 1].to_broadcast([P, P]))
                mm.then_inc(s_keys_ps, 1)

            def sum_same(n, valid):
                if not valid:
                    return
                pe.wait_ge(s_eq, n.n + 1)
                pe.wait_ge(s_val, n.n + 1)
                after(pe, s_sum, n.n)
                for i in range(2):
                    for j in range(2):
                        mm = pe.matmul(eH_ps[:, (2 + i) * P:(3 + i) * P], eq[:, j, i * P:i * P + P],
                                       val[n.slot][:, j, :], start=(j == 0), stop=(j == 1))
                mm.then_inc(s_sum_ps, 1)

            def d_transpose_x(g):
                if not g.within(0, NG):
                    return
                pe.wait_ge(d_x[g.slot], g.times(16))
                after(pe, d_x1T, g.n - 1)
                for t in range(4):
                    mm = transpose(dT_ps[:, t * P:t * P + P], dx[g.slot][:, t, :])
                mm.then_inc(d_xT_ps, 1)

            def d_root(g):
                if not g.within(0, NG):
                    return
                pe.wait_ge(d_xT, g.n + 1)
                after(pe, d_s, g.n)
                for t in range(4):
                    pe.matmul(dY_ps[:, t * D:t * D + D], dxT[:, t * P:t * P + P], w_root[:, :],
                                   start=(t == 0), stop=False, skip_group_check=True)
                mm = pe.matmul(dY_ps[:, :], ones3[:, :], bias[:, 0, :, :].rearrange("k t d -> k (t d)"), start=False, stop=True,
                               skip_group_check=True)
                mm.then_inc(d_y_ps, 1)

            def d_transpose_x1(g):
                if not g.within(0, NG):
                    return
                pe.wait_ge(d_x1, g.n + 1)
                pe.wait_ge(d_xT, g.n + 2 if g.back(-1).within(0, NG) else g.n + 1)
                for t in range(4):
                    mm = transpose(dT_ps[:, t * P:t * P + P], dx1[g.slot][:, t, :])
                mm.then_inc(d_x1T_ps, 1)

            def d_update1(g, last=NG, agg=False):
                if not g.within(0, last):
                    return
                pe.wait_ge(d_x1T, g.n + 1)
                after(pe, d_uT, g.n)
                mm = pe.matmul(dU_ps[:, :], u1[:, 0, :], dx1T[:, :], start=True, stop=not agg)
                if agg:
                    pe.wait_ge(q_aT, g.n - NG + 1)
                    mm = pe.matmul(dU_ps[:, :], u1[:, 1, :], daT[:, :], start=False, stop=True)
                mm.then_inc(d_u_ps, 1)

            def d_update2(g, last=NG):
                if not g.within(0, last):
                    return
                pe.wait_ge(d_uT, g.n + 1)
                after(pe, d_t, g.n)
                for t in range(4):
                    pe.matmul(dV_ps[:, t * D:t * D + D], duT[g.slot][:, t * P:t * P + P], u2c[:, :],
                                   start=(t == 0), stop=False, skip_group_check=True)
                mm = pe.matmul(dV_ps[:, :], ones3[:, :], bias[:, 2, :, :].rearrange("k t d -> k (t d)"), start=False, stop=True,
                               skip_group_check=True)
                mm.then_inc(d_v_ps, 1)

            def phase2(b):
                n = b.back(1)
                dense = b.within(0, NB)
                if dense:
                    d_transpose_x(b)
                sum_keys(n, n.within(0, NB))
                if dense:
                    d_root(b)
                    d_transpose_x1(b.back(1))
                    d_update1(b.back(1))
                sum_same(n, n.within(0, NB))
                if dense:
                    d_update2(b.back(1))

            pe.wait_ge(load_w, 16 * 9)
            pe.wait_ge(load_p, 16 * 4)
            pe.wait_ge(c_weights, 1)
            each(pe, NB + 1, 6, 1, phase2)

            def e_transpose_x(b):
                if not b.within(0, NB):
                    return
                pe.wait_ge(e_x[b.slot], b.times(32))
                after(pe, e_attrT, b.n - 1)
                for t in range(4):
                    mm = transpose(eT_ps[:, t * P:t * P + P], ex[b.slot][:, t, :])
                mm.then_inc(e_xT_ps, 1)

            def e_root(b):
                if not b.within(0, NB):
                    return
                pe.wait_ge(e_xT, b.n + 1)
                after(pe, e_v, b.n)
                for t in range(4):
                    pe.matmul(eY_ps[:, t * D:t * D + D], exT[:, t * P:t * P + P], w_root[:, :],
                                   start=(t == 0), stop=False, skip_group_check=True)
                mm = pe.matmul(eY_ps[:, :], ones3[:, :], bias[:, 0, :, :].rearrange("k t d -> k (t d)"), start=False, stop=True,
                               skip_group_check=True)
                mm.then_inc(e_y_ps, 1)

            def e_transpose_x1(b):
                if not b.within(0, NB):
                    return
                pe.wait_ge(e_x1, b.n + 1)
                pe.wait_ge(e_xT, b.n + 2 if b.back(-1).within(0, NB) else b.n + 1)
                for t in range(4):
                    mm = transpose(eT_ps[:, t * P:t * P + P], ex1[b.slot][:, t, :])
                mm.then_inc(e_x1T_ps, 1)

            def e_transpose_attr(b):
                if not b.within(0, NB):
                    return
                pe.wait_ge(e_attr[b.slot], b.times(16))
                pe.wait_ge(e_x1T, b.n + 1)
                for t in range(2):
                    mm = transpose(eT_ps[:, t * P:t * P + P], attr[b.slot][:, t, :])
                mm.then_inc(e_attrT_ps, 1)

            def e_message1(b):
                if not b.within(0, NB):
                    return
                pe.wait_ge(e_attrT, b.n + 1)
                after(pe, e_hT, b.n)
                pe.wait_ge(s_sum, b.n + NB)
                pe.matmul(eH_ps[:, 0:2 * P], m1[:, 0, :], ex1T[:, 0:2 * P], start=True, stop=False)
                pe.matmul(eH_ps[:, 0:2 * P], m1[:, 1, :], ex1T[:, 2 * P:4 * P], start=False, stop=False)
                pe.matmul(eH_ps[:, 0:2 * P], m1[:, 2, :], attrT[:, :], start=False, stop=True).then_inc(e_h_ps, 1)

            def e_message2(b):
                if not b.within(0, NB):
                    return
                pe.wait_ge(e_hT, b.n + 1)
                pe.wait_ge(s_eq, b.n + NB + 1)
                for t in range(2):
                    pe.matmul(eM_ps[:, t * D:t * D + D], hT[b.slot][:, t * P:t * P + P], m2[:, :],
                                   start=(t == 0), stop=False, skip_group_check=True)
                mm = pe.matmul(eM_ps[:, 0:2 * D], ones3[:, :], bias[:, 1, 0:2, :].rearrange("k t d -> k (t d)"), start=False, stop=True,
                               skip_group_check=True)
                mm.then_inc(e_m_ps, 1)

            def phase3(b):
                i = b.back(-NB)
                m = b.back(2)
                n, valid = m.back(-NB), m.within(0, NB)
                e_transpose_attr(m)
                d_transpose_x(i)
                e_message2(b.back(3))
                e_transpose_x(b)
                d_root(i)
                d_transpose_x1(i.back(1))
                sum_same(n.back(1), b.back(3).within(0, NB))
                e_root(b)
                d_update1(i.back(1))
                e_transpose_x1(b.back(1))
                e_message1(m)
                sum_keys(n, valid)
                d_update2(i.back(1))

            each(pe, NB + 3, 6, 5, phase3)

            def q_transposes(q):
                if not q.within(0, NQ):
                    return
                g = q.back(-NG)
                pe.wait_ge(q_agg[q.slot], q.times(64))
                after(pe, q_aT, q.n)
                for t in range(4):
                    mm = transpose(eT_ps[:, t * P:t * P + P], ea[q.slot][:, t, :])
                mm.then_inc(q_aT_ps, 1)
                pe.wait_ge(q_x1[g.slot], q.times(16))
                pe.wait_ge(d_x1T, g.n)
                for t in range(4):
                    mm = transpose(dT_ps[:, t * P:t * P + P], dx1[g.slot][:, t, :])
                mm.then_inc(d_x1T_ps, 1)

            def o_transpose_keys(q):
                if not q.within(0, NQ):
                    return
                pe.wait_ge(o_keys, q.n + 1)
                after(pe, o_same, q.n)
                for j in range(2):
                    mm = transpose(eM_ps[:, j * P:j * P + P], okey[q.slot][:, j:j + 1].to_broadcast([P, P]))
                mm.then_inc(o_keys_ps, 1)

            def phase4(k):
                o_transpose_keys(k.back(2))
                if k.back(1).within(0, NQ):
                    d_update2(k.back(1).back(-NG), NG + NQ)
                q_transposes(k)
                if k.within(0, NQ):
                    d_update1(k.back(-NG), NG + NQ, True)

            each(pe, NQ + 2, 6, 3, phase4)

        @block.scalar
        def _(act):
            def copy(dst, src):
                return act.activation(dst, src, ACT.Copy)

            def copy_keys(b):
                if not b.within(0, NB):
                    return
                act.wait_ge(a_keys_ps, b.n + 1)
                after(act, a_put, b.n - 1)
                after(act, a_distance, b.n - 1)
                copy(key_cols[b.slot], keys_ps[b.slot][:, :]).then_inc(a_key_cols, 1)

            def copy_types_and_x(b):
                if not b.within(0, NB):
                    return
                act.wait_ge(a_xsT_ps, b.n + 1)
                after(act, a_masked, (b.n - 1) * (R // 4))
                copy(cols[b.slot][:, :], typ_ps[b.slot][:, :]).then_inc(a_cols, 1)

            def key_distances(b):
                if not b.within(0, NB):
                    return
                act.wait_ge(a_key_cols, b.n + 1)
                after(act, a_cnt, b.n)
                for j in range(2):
                    ins = act.activation(distance[:, j, :], key_cols[b.slot][:, 0:2 * P], ACT.Square,
                                         bias=key[b.slot][:, SEG + j:SEG + j + 1], scale=-1.0)
                ins.then_inc(a_distance, 1)

            def count_same(b):
                if not b.within(0, NB):
                    return
                act.wait_ge(a_distance, b.n + 1)
                after(act, a_counted, (b.n - 1) * 32)
                for j in range(2):
                    ins = act.activation(same[:, j, :], distance[:, j, :], ACT.Relu, bias=one[:, 0:1], scale=-2.0,
                                         accum_out=cnt_new[b.slot][:, j:j + 1])
                ins.then_inc(a_cnt, 1)

            def copy_y(b):
                if not b.within(0, NB):
                    return
                act.wait_ge(a_y_ps, b.n + 1)
                copy(y_all[:, bass.ds(b.n * 2, 2), :].rearrange("p t d -> p (t d)"), y_ps[b.slot][:, 0:2 * D]).then_inc(a_y, 1)

            def columns(b):
                copy_keys(b)
                copy_types_and_x(b)
                key_distances(b)
                count_same(b)

            def phase1(b):
                columns(b.back(-1))
                copy_y(b.back(1))

            act.wait_ge(c_pool, 5)
            columns(At(0, 0))
            each(act, NB + 1, 4, 3, phase1)

            def copy_sum(n, valid):
                if not valid:
                    return
                act.wait_ge(s_sum_ps, n.n + 1)
                after(act, s_added, (n.n - 1) * 32)
                copy(flat_rows(put[n.slot]), eH_ps[:, 2 * P:4 * P]).then_inc(s_sum, 1)

            def d_root1(g):
                if not g.within(0, NG):
                    return
                act.wait_ge(d_mv1s, g.n + 1)
                after(act, d_rs1, g.n)
                act.activation(d_small[:, SD1, :], d_mv1[g.slot][:, :, 1], ACT.Sqrt, bias=eps[:, 0:1]).then_inc(d_sd1, 1)

            def d_norm1(g):
                if not g.within(0, NG):
                    return
                act.wait_ge(d_nm1, g.n + 1)
                after(act, d_x1b, g.n - 1)
                after(act, d_t, g.n - 1)
                after(act, d_x1T_ps, g.n - 1)
                for t in range(4):
                    ins = act.activation(dx1[g.slot][:, t, :], ds[g.slot][:, t, :], ACT.Identity,
                                         bias=d_small[:, NM1, t:t + 1], scale=d_small[:, RS1, t:t + 1])
                ins.then_inc(d_x1, 1)

            def d_copy_xT(g):
                if not g.within(0, NG):
                    return
                act.wait_ge(d_xT_ps, g.n + 1)
                after(act, d_y_ps, g.n)
                copy(dxT[:, :], dT_ps[:, :]).then_inc(d_xT, 1)

            def d_copy_x1T(g, last=NG):
                if not g.within(0, last):
                    return
                act.wait_ge(d_x1T_ps, g.n + 1)
                after(act, d_u_ps, g.n)
                copy(dx1T[:, :], dT_ps[:, :]).then_inc(d_x1T, 1)

            def d_relu(g, last=NG):
                if not g.within(0, last):
                    return
                act.wait_ge(d_u_ps, g.n + 1)
                after(act, d_v_ps, g.n - 1)
                act.activation(duT[g.slot][:, :], dU_ps[:, :], ACT.Relu, bias=u1_b[:, 0:1]).then_inc(d_uT, 1)

            def d_root2(g, last=NG):
                if not g.within(0, last):
                    return
                act.wait_ge(d_t, g.n + 1)
                after(act, d_sd2, g.n)
                for t in range(4):
                    ins = act.activation(d_junk[:, t, :], dt[:, t, :], ACT.Square, accum_out=d_small[:, SS2, t:t + 1])
                ins.then_inc(d_ss2, 1)
                act.wait_ge(d_ss2, g.n + 1)
                after(act, d_rs2, g.n)
                act.activation(d_small[:, SD2, :], d_small[:, SS2, :], ACT.Sqrt, bias=eps[:, 0:1], scale=1.0 / D).then_inc(d_sd2, 1)

            def d_root3(g, last=NG):
                if not g.within(0, last):
                    return
                act.wait_ge(d_mv3s, g.n + 1)
                after(act, d_rs3, g.n)
                act.activation(d_small[:, SD3, :], d_mv3[:, :, 1], ACT.Sqrt, bias=eps[:, 0:1]).then_inc(d_sd3, 1)

            def d_norm3(g, last=NG):
                if not g.within(0, last):
                    return
                act.wait_ge(d_nm3, g.n + 1)
                if last == NG:
                    if g.back(2).within(0, last):
                        act.wait_ge(d_stored[g.slot], g.back(2).times(16))
                else:
                    after(act, q_out, (g.n - NG - 1) * 64)
                for t in range(4):
                    ins = act.activation(do[g.slot][:, t, :], dr[g.slot][:, t, :], ACT.Identity,
                                         bias=d_small[:, NM3, t:t + 1], scale=d_small[:, RS3, t:t + 1])
                ins.then_inc(d_o, 1)

            def phase2(b):
                n = b.back(1)
                if b.within(0, NB):
                    d_copy_xT(b)
                    d_norm1(b.back(1))
                    d_root3(b.back(3))
                    d_copy_x1T(b.back(1))
                    d_root2(b.back(2))
                    d_relu(b.back(1))
                    d_root1(b)
                    d_norm3(b.back(3))
                copy_sum(n, n.within(0, NB))

            each(act, NB + 1, 6, 1, phase2)

            def e_root(b):
                if not b.within(0, NB):
                    return
                act.wait_ge(e_mvs, b.n + 1)
                after(act, e_rs, b.n)
                act.activation(e_small[:, 0, :], e_mv[b.slot][:, :, 1], ACT.Sqrt, bias=eps[:, 0:1]).then_inc(e_sd, 1)

            def e_copy_xT(b):
                if not b.within(0, NB):
                    return
                act.wait_ge(e_xT_ps, b.n + 1)
                after(act, e_y_ps, b.n)
                copy(exT[:, :], eT_ps[:, :]).then_inc(e_xT, 1)

            def e_copy_message(b):
                if not b.within(0, NB):
                    return
                act.wait_ge(e_m_ps, b.n + 1)
                after(act, s_sum_ps, b.n + NB - 1)
                copy(flat_rows(val[b.slot]), eM_ps[:, 0:2 * D]).then_inc(s_val, 1)

            def e_copy_x1T(b):
                if not b.within(0, NB):
                    return
                act.wait_ge(e_x1T_ps, b.n + 1)
                after(act, e_h_ps, b.n)
                copy(ex1T[:, :], eT_ps[:, :]).then_inc(e_x1T, 1)

            def e_copy_attrT(b):
                if not b.within(0, NB):
                    return
                act.wait_ge(e_attrT_ps, b.n + 1)
                copy(attrT[:, :], eT_ps[:, 0:2 * P]).then_inc(e_attrT, 1)

            def e_relu(b):
                if not b.within(0, NB):
                    return
                act.wait_ge(e_h_ps, b.n + 1)
                after(act, e_m_ps, b.n - 1)
                act.activation(hT[b.slot][:, :], eH_ps[:, 0:2 * P], ACT.Relu, bias=m1_b[:, 0:1]).then_inc(e_hT, 1)

            def phase3(b):
                i = b.back(-NB)
                m = b.back(3)
                e_copy_attrT(b.back(2))
                d_copy_xT(i)
                d_norm1(i.back(1))
                e_copy_message(m)
                e_copy_xT(b)
                e_root(b.back(1))
                d_copy_x1T(i.back(1))
                copy_sum(m.back(-NB), m.within(0, NB))
                d_root3(i.back(3))
                d_root2(i.back(2))
                d_relu(i.back(1))
                d_norm3(i.back(3))
                e_copy_x1T(b.back(1))
                e_relu(b.back(2))
                d_root1(i)

            each(act, NB + 3, 6, 5, phase3)

            def phase4(k):
                g = k.back(-NG)
                last = NG + NQ
                if k.back(3).within(0, NQ):
                    d_root3(g.back(3), last)
                    d_norm3(g.back(3), last)
                if k.back(1).within(0, NQ):
                    d_relu(g.back(1), last)
                if k.within(0, NQ):
                    act.wait_ge(q_aT_ps, k.n + 1)
                    after(act, d_u_ps, g.n)
                    copy(daT[:, :], eT_ps[:, :]).then_inc(q_aT, 1)
                if k.back(1).within(0, NQ):
                    d_root2(g.back(1), last)
                if k.within(0, NQ):
                    d_copy_x1T(g, last)

            for s in range(2):
                act.wait_ge(d_stored[s], 16 * (NG // 2))
            each(act, NQ + 3, 6, 3, phase4)

        @block.vector
        def _(dve):
            tt, stt, ts, cp = dve.tensor_tensor, dve.scalar_tensor_tensor, dve.tensor_scalar, dve.tensor_copy
            chain = [0]

            def link(ins):
                chain[0] += 1
                ins.then_inc(c_dve, 1)
                dve.wait_ge(c_dve, chain[0])

            dve.wait_ge(load_i, 16 * 6)
            for q, row in ((0, 0), (1, 2), (2, 3)):
                ins = cp(key_rows[:, row, :], idx_rows[:, q, :])
            link(ins)
            stt(out=key_rows[:, 1, :], in0=key_rows[:, 2, :], scalar=float(R), in1=key_rows[:, 3, :],
                op0=ALU.mult, op1=ALU.add).then_inc(c_key, 1)
            dve.wait_ge(c_keyT, 1)
            for h in range(2):
                ins = cp(keys[:, :, 4 * h:4 * h + 4].rearrange("p b k -> p k b"),
                         bank[h][:, 0:4 * NB].rearrange("p (k b) -> p k b", b=NB))
            ins.then_inc(c_cols, 1)
            dve.wait_ge(c_cols, 1)
            dve.wait_ge(c_pool, 5)
            cp(pair_f[:, :], pair[:, :])
            link(cp(dump[:, :], dump_i[:, :]))
            if REPEATED:
                ts(keys[0:REPEATED, NB - 1, SEG:SEG + 2], pair_f[0:REPEATED, :], float(SEGS), None, ALU.add)
                link(ts(keys[0:REPEATED, NB - 1, DST:DST + 2], pair_f[0:REPEATED, :], float(N), None, ALU.add))
            cp(index[:, :, I_SRC:I_SRC + 2], keys[:, :, SRC:SRC + 2])
            ts(index[:, :, I_DSTX:I_DSTX + 2], keys[:, :, DST:DST + 2], float(N - 1), None, ALU.min)
            link(cp(index[:, :, I_SEG:I_SEG + 4], keys[:, :, SEG:SEG + 4]))

            tt(to_dump[:, :, :], dump[:, :].unsqueeze(1).to_broadcast([P, NB, 4]), keys[:, :, SEG:SEG + 4], ALU.subtract)

            def stage_index(b):
                if not b.within(0, NB):
                    return
                if b.back(2).within(0, NB):
                    dve.wait_ge(a_src[b.slot], b.back(2).times(32))
                    dve.wait_ge(a_dst[b.slot], b.back(2).times(32))
                cp(idx[b.slot][:, 0:4], index[:, b.n, 0:4]).then_inc(a_idx, 1)

            def stage_key(b):
                if not b.within(0, NB):
                    return
                after(dve, a_xsT_ps, b.n - 1)
                after(dve, a_put, b.n - 1)
                after(dve, a_distance, b.n - 1)
                cp(key[b.slot][:, :], keys[:, b.n, :]).then_inc(a_staged, 1)

            def mask(b, types):
                if not b.within(0, NB):
                    return
                dve.wait_ge(a_cols, b.n + 1)
                after(dve, a_y_ps, b.n - 1)
                for r in types:
                    ins = stt(out=masked[b.slot][:, r, :], in0=cols[b.slot][:, 0:2 * P], scalar=float(r),
                              in1=cols[b.slot][:, 2 * P:4 * P], op0=ALU.is_equal, op1=ALU.mult)
                    if r % 4 == 3:
                        ins.then_inc(a_masked, 1)

            def find_earlier(b):
                if not b.within(0, NB):
                    return
                k, ps = key[b.slot], key_cols[b.slot]
                dve.wait_ge(a_key_cols, b.n + 1)
                after(dve, a_put, b.n)
                for w, at in ((0, SEG), (1, DST)):
                    stt(out=same[:, 2 + 2 * w, 0:P], in0=ps[:, 2 * w * P:(2 * w + 1) * P], scalar=k[:, at:at + 1],
                        in1=earlier[:, 1, :], op0=ALU.is_equal, op1=ALU.mult, accum_out=dup[:, 2 * w:2 * w + 1])
                    ins = stt(out=same[:, 3 + 2 * w, :], in0=ps[:, 2 * w * P:(2 * w + 2) * P], scalar=k[:, at + 1:at + 2],
                        in1=earlier[:, :, :].rearrange("p i k -> p (i k)"), op0=ALU.is_equal, op1=ALU.mult,
                        accum_out=dup[:, 2 * w + 1:2 * w + 2])
                ins.then_inc(a_same, 1)

            def place(b):
                if not b.within(0, NB):
                    return
                k = key[b.slot]
                dve.wait_ge(a_same, b.n + 1)
                stt(out=moved[:, :], in0=dup[:, :], scalar=0.0, in1=to_dump[:, b.n, :],
                    op0=ALU.is_gt, op1=ALU.mult).then_inc(a_dup, 1)
                dve.wait_ge(a_dup, b.n + 1)
                after(dve, a_counted, (b.n - 1) * 32)
                tt(put_cnt[b.slot][:, :], moved[:, 0:2], k[:, SEG:SEG + 2], ALU.add)
                tt(index[:, b.n, I_PUT:I_PUT + 2], moved[:, 2:4], k[:, DST:DST + 2], ALU.add).then_inc(a_put, 1)

            def phase1(b):
                mask(b, range(0, 4))
                place(b.back(1))
                stage_key(b.back(-1))
                mask(b, range(4, R))
                stage_index(b.back(-2))
                find_earlier(b)

            for n in range(2):
                stage_index(At(0, n))
            stage_key(At(0, 0))
            each(dve, NB + 1, 4, 3, phase1)

            def stage_sum(n, b, valid):
                if not valid:
                    return
                after(dve, s_eq, n.n - 1)
                after(dve, s_added, (n.n - 1) * 32)
                cp(pkey[n.slot][:, :], keys[:, b.n, DST:DST + 2])
                cp(pidx[n.slot][:, :], index[:, b.n, I_PUT:I_PUT + 2]).then_inc(s_staged, 1)

            def equal(n, valid):
                if not valid:
                    return
                dve.wait_ge(s_keys_ps, n.n + 1)
                after(dve, s_sum_ps, n.n)
                for j in range(2):
                    ins = ts(eq[:, j, :], eM_ps[:, 2 * P:4 * P], pkey[n.slot][:, j:j + 1], None, ALU.is_equal)
                ins.then_inc(s_eq, 1)

            def stage2(b):
                if not b.within(0, NB):
                    return
                if b.back(2).within(0, NB):
                    dve.wait_ge(b_cnt[b.slot], b.back(2).times(32))
                cp(idx[b.slot][:, I_SEG:I_SEG + 2], index[:, b.n, I_SEG:I_SEG + 2]).then_inc(b_staged, 1)

            def at_least_1(b):
                if not b.within(0, NB):
                    return
                dve.wait_ge(b_cnt[b.slot], b.times(32))
                after(dve, s_val, b.n)
                ts(inv[:, 0, :], cnt[b.slot][:, :], 1.0, None, ALU.max).then_inc(b_max, 1)

            def invert(b):
                if not b.within(0, NB):
                    return
                dve.wait_ge(b_max, b.n + 1)
                dve.reciprocal(inv[:, 1, :], inv[:, 0, :]).then_inc(b_inv, 1)

            def weigh(b):
                if not b.within(0, NB):
                    return
                dve.wait_ge(b_inv, b.n + 1)
                after(dve, s_sum_ps, b.n - 1)
                tt(val[b.slot][:, :, :], y_all[:, bass.ds(b.n * 2, 2), :],
                   inv[:, 1, :].unsqueeze(2).to_broadcast([P, 2, D]), ALU.mult).then_inc(s_val, 1)

            def d_inverse1(g):
                if not g.within(0, NG):
                    return
                dve.wait_ge(d_sd1, g.n + 1)
                after(dve, d_x1, g.n)
                dve.reciprocal(d_small[:, RS1, :], d_small[:, SD1, :]).then_inc(d_rs1, 1)

            def d_shift1(g):
                if not g.within(0, NG):
                    return
                dve.wait_ge(d_rs1, g.n + 1)
                after(dve, d_x1, g.n)
                stt(out=d_small[:, NM1, :], in0=d_mv1[g.slot][:, :, 0], scalar=-1.0, in1=d_small[:, RS1, :],
                    op0=ALU.mult, op1=ALU.mult).then_inc(d_nm1, 1)

            def d_sum(g):
                if not g.within(0, NG):
                    return
                dve.wait_ge(d_y_ps, g.n + 1)
                after(dve, d_x1, g.n - 1)
                stt(out=ds[g.slot], in0=bank4(dY_ps), scalar=0.0, in1=dx[g.slot], op0=ALU.max, op1=ALU.add).then_inc(d_s, 1)

            def d_bn1(g):
                if not g.within(0, NG):
                    return
                dve.wait_ge(d_s, g.n + 1)
                after(dve, d_mv1s, g.n)
                for t in range(4):
                    ins = dve.bn_stats(d_st[:, 0, t, :], ds[g.slot][:, t, :])
                ins.then_inc(d_stats1, 1)

            def d_aggr1(g):
                if not g.within(0, NG):
                    return
                dve.wait_ge(d_stats1, g.n + 1)
                after(dve, d_nm1, g.n - 1)
                apart(dve)
                for t in range(4):
                    ins = dve.bn_aggr(d_mv1[g.slot][:, t, :], d_st[:, 0, t, :])
                ins.then_inc(d_mv1s, 1)

            def d_add2(g, last=NG):
                if not g.within(0, last):
                    return
                dve.wait_ge(d_v_ps, g.n + 1)
                after(dve, d_qg, g.n)
                tt(dt[:, :, :], bank4(dV_ps), dx1[g.slot], ALU.add).then_inc(d_t, 1)

            def d_inverse2(g, last=NG):
                if not g.within(0, last):
                    return
                dve.wait_ge(d_sd2, g.n + 1)
                after(dve, d_qg, g.n)
                dve.reciprocal(d_small[:, RS2, :], d_small[:, SD2, :]).then_inc(d_rs2, 1)

            def d_gamma(g, last=NG):
                if not g.within(0, last):
                    return
                dve.wait_ge(d_rs2, g.n + 1)
                after(dve, d_r, g.n)
                for t in range(4):
                    ins = stt(out=dq[:, t, :], in0=dt[:, t, :], scalar=d_small[:, RS2, t:t + 1], in1=gamma[:, :],
                              op0=ALU.mult, op1=ALU.mult)
                ins.then_inc(d_qg, 1)

            def q_residual(g):
                dve.wait_ge(d_qg, g.n + 1)
                dve.wait_ge(d_x1b, g.n + 1)
                after(dve, d_o, g.n - 1)
                tt(dr[g.slot], dq[:, :, :], dx1b[:, :, :], ALU.add).then_inc(d_r, 1)

            def d_bn3(g, last=NG):
                if not g.within(0, last):
                    return
                dve.wait_ge(d_r, g.n + 1)
                after(dve, d_mv3s, g.n)
                for t in range(4):
                    ins = dve.bn_stats(d_st[:, 1, t, :], dr[g.slot][:, t, :])
                ins.then_inc(d_stats3, 1)

            def d_aggr3(g, last=NG):
                if not g.within(0, last):
                    return
                dve.wait_ge(d_stats3, g.n + 1)
                after(dve, d_nm3, g.n)
                apart(dve)
                for t in range(4):
                    ins = dve.bn_aggr(d_mv3[:, t, :], d_st[:, 1, t, :])
                ins.then_inc(d_mv3s, 1)

            def d_inverse3(g, last=NG):
                if not g.within(0, last):
                    return
                dve.wait_ge(d_sd3, g.n + 1)
                after(dve, d_o, g.n)
                dve.reciprocal(d_small[:, RS3, :], d_small[:, SD3, :]).then_inc(d_rs3, 1)

            def d_shift3(g, last=NG):
                if not g.within(0, last):
                    return
                dve.wait_ge(d_rs3, g.n + 1)
                stt(out=d_small[:, NM3, :], in0=d_mv3[:, :, 0], scalar=-1.0, in1=d_small[:, RS3, :],
                    op0=ALU.mult, op1=ALU.mult).then_inc(d_nm3, 1)

            def phase2(b):
                n = b.back(1)
                valid, dense = n.within(0, NB), b.within(0, NB)
                if dense:
                    d_gamma(b.back(3))
                    d_inverse1(b.back(1))
                stage_sum(n, n, valid)
                if dense:
                    d_shift1(b.back(1))
                    d_add2(b.back(2))
                equal(n, valid)
                at_least_1(n)
                if dense:
                    d_bn3(b.back(3))
                invert(n)
                if dense:
                    d_aggr3(b.back(3))
                    d_sum(b)
                stage2(b)
                if dense:
                    d_inverse3(b.back(3))
                weigh(n)
                if dense:
                    d_bn1(b)
                    d_shift3(b.back(3))
                    d_aggr1(b)
                    d_inverse2(b.back(2))

            dve.wait_ge(load_w, 16 * 9)
            dve.wait_ge(load_b, 16 * 3)
            dve.bn_stats(w_stats[:, 0, :], u2[:, :])
            link(dve.bn_stats(w_stats[0:1, 1, :], b_row[:, 2, :]))
            dve.bn_aggr(w_mean[:, 0, :], w_stats[:, 0, :])
            link(dve.bn_aggr(w_mean[0:1, 1, :], w_stats[0:1, 1, :]))
            ts(u2c[:, :], u2[:, :], w_mean[:, 0, 0:1], None, ALU.subtract).then_inc(c_weights, 1)
            link(ts(b_row[:, 2, :], b_row[:, 2, :], w_mean[0:1, 1, 0:1], None, ALU.subtract))
            for k in range(3):
                link(cp(b_parts[:, k, :, :], b_row[:, :, :]))
                if k < 2:
                    link(cp(b_back[:, :, :], b_parts[:, k, :, :]))
                    link(tt(b_row[:, :, :], b_row[:, :, :], b_back[:, :, :], ALU.subtract))
            dve.engine_nop().then_inc(c_parts, 1)

            dve.wait_ge(a_put, NB)
            dve.wait_ge(a_cnt, NB)
            dve.wait_ge(a_src[0], 16 * NB)
            dve.wait_ge(a_src[1], 16 * NB)
            dve.wait_ge(a_dst[0], 16 * NB)
            dve.wait_ge(a_dst[1], 16 * NB)
            dve.wait_ge(a_y, NB)
            each(dve, NB + 1, 6, 1, phase2)

            def stage3(b):
                if not b.within(0, NB):
                    return
                if b.back(2).within(0, NB):
                    dve.wait_ge(e_agg[b.slot], b.back(2).times(64))
                cp(idx[b.slot][:, :], index[:, b.n, :]).then_inc(e_staged, 1)

            def e_scale(b):
                if not b.within(0, NB):
                    return
                dve.wait_ge(e_sd, b.n + 1)
                after(dve, e_x1, b.n)
                dve.reciprocal(e_small[:, 1, :], e_small[:, 0, :]).then_inc(e_rs, 1)

            def e_norm(b):
                if not b.within(0, NB):
                    return
                dve.wait_ge(e_rs, b.n + 1)
                if b.back(2).within(0, NB):
                    dve.wait_ge(e_kept[b.slot], b.back(2).times(16))
                    dve.wait_ge(e_x1T_ps, b.n - 1)
                for t in range(4):
                    ins = ts(ex1[b.slot][:, t, :], es[b.slot][:, t, :], e_mv[b.slot][:, t, 0:1], e_small[:, 1, t:t + 1],
                             ALU.subtract, ALU.mult)
                ins.then_inc(e_x1, 1)

            def e_add(b):
                if not b.within(0, NB):
                    return
                dve.wait_ge(e_y_ps, b.n + 1)
                dve.wait_ge(e_agg[b.slot], b.times(64))
                after(dve, e_x1, b.n - 1)
                tt(es[b.slot], bank4(eY_ps), ea[b.slot], ALU.add).then_inc(e_v, 1)

            def e_sum(b):
                if not b.within(0, NB):
                    return
                dve.wait_ge(e_v, b.n + 1)
                stt(out=es[b.slot], in0=es[b.slot], scalar=0.0, in1=ex[b.slot], op0=ALU.max, op1=ALU.add).then_inc(e_s, 1)

            def e_bn(b):
                if not b.within(0, NB):
                    return
                dve.wait_ge(e_s, b.n + 1)
                after(dve, e_mvs, b.n)
                for t in range(4):
                    ins = dve.bn_stats(e_st[:, t, :], es[b.slot][:, t, :])
                ins.then_inc(e_stats, 1)

            def e_aggr(b):
                if not b.within(0, NB):
                    return
                dve.wait_ge(e_stats, b.n + 1)
                after(dve, e_x1, b.n - 1)
                apart(dve)
                for t in range(4):
                    ins = dve.bn_aggr(e_mv[b.slot][:, t, :], e_st[:, t, :])
                ins.then_inc(e_mvs, 1)

            def phase3(b):
                i = b.back(-NB)
                m = b.back(2)
                equal(i.back(3), b.back(3).within(0, NB))
                d_gamma(i.back(3))
                d_inverse1(i.back(1))
                stage_sum(m.back(-NB), m, m.within(0, NB))
                d_shift1(i.back(1))
                stage3(b.back(-1))
                e_bn(b.back(1))
                d_add2(i.back(2))
                e_aggr(b.back(1))
                d_bn3(i.back(3))
                d_sum(i)
                e_scale(b.back(1))
                d_aggr3(i.back(3))
                e_norm(b.back(1))
                d_bn1(i)
                d_inverse3(i.back(3))
                d_aggr1(i)
                d_shift3(i.back(3))
                d_inverse2(i.back(2))
                e_add(b)
                e_sum(b)

            for s in range(2):
                dve.wait_ge(b_cnt[s], 16 * NB)
            stage3(At(0, 0))
            each(dve, NB + 3, 6, 5, phase3)

            def stage4(q):
                if not q.within(0, NQ):
                    return
                if q.back(2).within(0, NQ):
                    dve.wait_ge(q_agg[q.slot], q.back(2).times(64))
                cp(qidx[q.slot][:, :, :], index[:, bass.ds(q.n * 2, 2), :]).then_inc(q_staged, 1)

            def stage_keys(q):
                if not q.within(0, NQ):
                    return
                after(dve, o_same, q.n - 1)
                cp(okey[q.slot][:, :].rearrange("p (b j) -> p b j", b=2),
                   keys[:, bass.ds(q.n * 2, 2), DST:DST + 2]).then_inc(o_keys, 1)

            def stage_out(q):
                if not q.within(0, NQ):
                    return
                dve.wait_ge(o_keys_ps, q.n + 1)
                after(dve, o_staged, q.n)
                cp(oput[:, :].rearrange("p (b j) -> p b j", b=2), index[:, bass.ds(q.n * 2, 2), I_PUT:I_PUT + 2])
                for j in range(2):
                    ins = ts(same[:, j, :], eM_ps[:, 0:2 * P], okey[q.slot][:, 2 + j:3 + j], 0.0, ALU.is_equal, ALU.add,
                             accum_out=odup[:, j:j + 1])
                ins.then_inc(o_same, 1)
                dve.wait_ge(o_same, q.n + 1)
                ts(omoved[:, :], odup[:, :], 0.0, float(TABLE), ALU.is_gt, ALU.mult).then_inc(o_moved, 1)
                dve.wait_ge(o_moved, q.n + 1)
                after(dve, q_out, (q.n - 1) * 64)
                cp(oidx[q.slot][:, 0:2], oput[:, 0:2])
                tt(oidx[q.slot][:, 2:4], omoved[:, :], oput[:, 2:4], ALU.add).then_inc(o_staged, 1)

            def q_beta(q):
                if not q.within(0, NQ):
                    return
                g = q.back(-NG)
                dve.wait_ge(q_x1[g.slot], q.times(16))
                after(dve, d_r, g.n)
                tt(dx1b[:, :, :], dx1[g.slot], beta[:, :].unsqueeze(1).to_broadcast([P, 4, D]), ALU.add).then_inc(d_x1b, 1)

            def phase4(k):
                g = k.back(-NG)
                last = NG + NQ
                if k.back(3).within(0, NQ):
                    d_bn3(g.back(3), last)
                stage_keys(k.back(2))
                if k.back(3).within(0, NQ):
                    d_aggr3(g.back(3), last)
                stage4(k)
                if k.back(3).within(0, NQ):
                    d_inverse3(g.back(3), last)
                if k.back(2).within(0, NQ):
                    d_inverse2(g.back(2), last)
                if k.back(3).within(0, NQ):
                    d_shift3(g.back(3), last)
                if k.back(2).within(0, NQ):
                    d_gamma(g.back(2), last)
                    q_residual(g.back(2))
                q_beta(k.back(1))
                stage_out(k.back(2))
                if k.back(1).within(0, NQ):
                    d_add2(g.back(1), last)

            each(dve, NQ + 3, 6, 3, phase4)


_INS = ["x", "src", "dst", "edge_attr_128", "edge_type_16", "L0_gnn_W_rel", "L0_gnn_W_root", "L0_gnn_bias",
        "L1_gnn_msg_W1", "L1_gnn_msg_b1", "L1_gnn_msg_W2", "L1_gnn_msg_b2", "L1_gnn_upd_W1", "L1_gnn_upd_b1",
        "L1_gnn_upd_W2", "L1_gnn_upd_b2", "L1_gnn_ln_gamma", "L1_gnn_ln_beta"]


def kernel(**inputs):
    import numpy as _np
    import concourse.bacc as _bacc
    from concourse import mybir as _mybir
    from concourse.bass_utils import run_bass_kernel_spmd as _run

    nc = _bacc.Bacc("TRN2", target_bir_lowering=False, num_devices=1)
    arrays, aps = {}, {}
    for name in _INS:
        a = _np.ascontiguousarray(inputs[name])
        arrays[f"in_{name}"] = a
        aps[name] = nc.dram_tensor(f"in_{name}", a.shape, _mybir.dt.from_np(a.dtype), kind="ExternalInput").ap()
    out = nc.dram_tensor("out_0", arrays["in_x"].shape, _mybir.dt.float32, kind="ExternalOutput").ap()
    build(nc, aps, out)
    r = _run(nc, [arrays], core_ids=[0])
    return r.results[0]["out_0"]
```
